# Optimizing a Trainium2 kernel written in Bass

```python
import numpy as np
import jax
import jax.numpy as jnp

def _softmax(x, axis=-1):
    return jax.nn.softmax(x, axis=axis)

def _gelu(x):
    return jax.nn.gelu(x, approximate=True)

def _silu(x):
    return jax.nn.silu(x)

def _sigmoid(x):
    return jax.nn.sigmoid(x)

def _layernorm(x, axis=-1, eps=1e-05):
    m = jnp.mean(x, axis=axis, keepdims=True)
    v = jnp.var(x, axis=axis, keepdims=True)
    return (x - m) / jnp.sqrt(v + eps)

def _scatter_add(tgt, idx, src, axis=0):
    return tgt.at[idx].add(src)

def _segment_sum(src, seg, n):
    return jax.ops.segment_sum(src, seg, n)
kernel_name = 'mk_early_fusion_embed_d2_tok_img768_r4_bc74f9'

def setup_inputs(seed: int=0):
    np.random.seed(seed)
    _w = jnp.asarray

    def _rec_inputs():
        import jax
        import jax.numpy as jnp
        _rk = jax.random.key(seed)
        x = 7.57192e-06 + 1.00007 * jax.random.normal(jax.random.fold_in(_rk, 1), (16, 3, 224, 224), jnp.float32)
        x_txt = jax.random.randint(jax.random.fold_in(_rk, 51), (16, 512), 0, 8000, jnp.int32)
        return (x, x_txt)
    x, x_txt = _rec_inputs()

    def _L0_tok_setup():
        import jax, jax.numpy as jnp
        import numpy as np
        K = 4
        STRIDE = 4
        EPS = 1e-05
        SLOPE = 0.01

        def conv2d(x, w, b, stride):
            out = jax.lax.conv_general_dilated(x, w, (stride, stride), 'VALID', dimension_numbers=('NCHW', 'OIHW', 'NCHW'))
            return out + b[None, :, None, None]

        def batchnorm(x, g, b, m, v):
            inv = g / jnp.sqrt(v + EPS)
            return x * inv[None, :, None, None] + (b - m * inv)[None, :, None, None]

        def leaky_relu(x):
            return jnp.where(x >= 0, x, SLOPE * x)

        def deform_conv(x, offset, w, b):
            B, C, H, W = x.shape
            Ho, Wo = (offset.shape[2], offset.shape[3])
            KK = K * K
            off = offset.reshape(B, KK, 2, Ho, Wo)
            kh = jnp.repeat(jnp.arange(K), K).astype(x.dtype)
            kw = jnp.tile(jnp.arange(K), K).astype(x.dtype)
            base_y = (jnp.arange(Ho) * STRIDE).astype(x.dtype)
            base_x = (jnp.arange(Wo) * STRIDE).astype(x.dtype)
            py = base_y[None, None, :, None] + kh[None, :, None, None] + off[:, :, 0]
            px = base_x[None, None, None, :] + kw[None, :, None, None] + off[:, :, 1]
            y0 = jnp.floor(py)
            x0 = jnp.floor(px)
            wy = py - y0
            wx = px - x0

            def corner(yc, xc):
                yi = yc.astype(jnp.int32)
                xi = xc.astype(jnp.int32)
                valid = (yi >= 0) & (yi < H) & (xi >= 0) & (xi < W)
                yi = jnp.clip(yi, 0, H - 1)
                xi = jnp.clip(xi, 0, W - 1)
                v = jax.vmap(lambda img, a, c: img[:, a, c])(x, yi, xi)
                return v * valid[:, None].astype(x.dtype)
            v00 = corner(y0, x0)
            v01 = corner(y0, x0 + 1)
            v10 = corner(y0 + 1, x0)
            v11 = corner(y0 + 1, x0 + 1)
            wy_ = wy[:, None]
            wx_ = wx[:, None]
            sampled = v00 * (1 - wy_) * (1 - wx_) + v01 * (1 - wy_) * wx_ + v10 * wy_ * (1 - wx_) + v11 * wy_ * wx_
            out = jnp.einsum('bckhw,ock->bohw', sampled, w.reshape(w.shape[0], C, KK))
            return out + b[None, :, None, None]
        key = jax.random.key(seed)
        ks = jax.random.split(key, 16)
        f32 = jnp.float32
        inp = {'x': jax.random.normal(ks[0], (64, 3, 224, 224), f32), 'stem_w': jax.random.normal(ks[1], (96, 3, 4, 4), f32) * 0.1, 'stem_b': jax.random.normal(ks[2], (96,), f32) * 0.05, 'bn1_g': jax.random.uniform(ks[3], (96,), f32, 0.5, 1.5), 'bn1_b': jax.random.normal(ks[4], (96,), f32) * 0.05, 'bn1_m': jax.random.normal(ks[5], (96,), f32) * 0.05, 'bn1_v': jax.random.uniform(ks[6], (96,), f32, 0.5, 1.5), 'off_w': jax.random.normal(ks[7], (32, 96, 4, 4), f32) * 0.02, 'off_b': jax.random.normal(ks[8], (32,), f32) * 0.02, 'dcn_w': jax.random.normal(ks[9], (192, 96, 4, 4), f32) * 0.05, 'dcn_b': jax.random.normal(ks[10], (192,), f32) * 0.05, 'bn2_g': jax.random.uniform(ks[11], (192,), f32, 0.5, 1.5), 'bn2_b': jax.random.normal(ks[12], (192,), f32) * 0.05, 'bn2_m': jax.random.normal(ks[13], (192,), f32) * 0.05, 'bn2_v': jax.random.uniform(ks[14], (192,), f32, 0.5, 1.5)}
        return inp
    _L0_tok_all = _L0_tok_setup()
    _L0_tok_in = {k: v for k, v in _L0_tok_all.items() if k in ('stem_w', 'stem_b', 'bn1_g', 'bn1_b', 'bn1_m', 'bn1_v', 'off_w', 'off_b', 'dcn_w', 'dcn_b', 'bn2_g', 'bn2_b', 'bn2_m', 'bn2_v')}
    del _L0_tok_all

    def _L0_txt_setup():
        import jax, jax.numpy as jnp
        import numpy as np
        N_QUBITS = 6
        N_LAYERS = 3
        DIM = 1 << N_QUBITS
        VOCAB = 8000
        EMBED = 192
        B, S = (16, 1024)

        def _cnot_perm(control, target):
            idx = np.arange(DIM)
            cbit = idx >> N_QUBITS - 1 - control & 1
            flipped = idx ^ 1 << N_QUBITS - 1 - target
            return np.where(cbit == 1, flipped, idx)
        _idx = np.arange(DIM)
        Z_SIGNS = np.stack([1.0 - 2.0 * (_idx >> N_QUBITS - 1 - q & 1) for q in range(N_QUBITS)], axis=1).astype(np.float32)

        def _apply_ry(state, theta, q):
            T = state.shape[0]
            left, right = (1 << q, 1 << N_QUBITS - 1 - q)
            s = state.reshape(T, left, 2, right)
            c = jnp.cos(theta * 0.5)[:, None, None]
            sn = jnp.sin(theta * 0.5)[:, None, None]
            a0, a1 = (s[:, :, 0, :], s[:, :, 1, :])
            out = jnp.stack([c * a0 - sn * a1, sn * a0 + c * a1], axis=2)
            return out.reshape(T, DIM)

        def _apply_rz(state, theta, q):
            T = state.shape[0]
            left, right = (1 << q, 1 << N_QUBITS - 1 - q)
            s = state.reshape(T, left, 2, right)
            ph = jnp.exp(1j * (theta * 0.5)).astype(state.dtype)[:, None, None]
            out = jnp.stack([jnp.conj(ph) * s[:, :, 0, :], ph * s[:, :, 1, :]], axis=2)
            return out.reshape(T, DIM)

        def _circuit_expvals(params):
            T = params.shape[0]
            state = jnp.zeros((T, DIM), dtype=jnp.complex64).at[:, 0].set(1.0)
            for layer in range(N_LAYERS):
                for q in range(N_QUBITS):
                    state = _apply_ry(state, params[:, layer, q, 0], q)
                    state = _apply_rz(state, params[:, layer, q, 1], q)
                if layer < N_LAYERS - 1:
                    for q in range(N_QUBITS - 1):
                        state = state[:, _cnot_perm(q, q + 1)]
                    if N_QUBITS > 2:
                        state = state[:, _cnot_perm(N_QUBITS - 1, 0)]
            probs = state.real ** 2 + state.imag ** 2
            return probs @ jnp.asarray(Z_SIGNS)
        key = jax.random.key(seed)
        k1, k2, k3, k4 = jax.random.split(key, 4)
        token_ids = jax.random.randint(k1, (B, S), 0, VOCAB)
        quantum_params = jax.random.normal(k2, (VOCAB, N_LAYERS, N_QUBITS, 2), dtype=jnp.float32) * 0.1
        post_w = jax.random.normal(k3, (EMBED, N_QUBITS), dtype=jnp.float32) / np.sqrt(N_QUBITS)
        post_b = jax.random.normal(k4, (EMBED,), dtype=jnp.float32) * 0.01
        return {'token_ids': token_ids, 'quantum_params': quantum_params, 'post_w': post_w, 'post_b': post_b}
    _L0_txt_all = _L0_txt_setup()
    _L0_txt_in = {k: v for k, v in _L0_txt_all.items() if k in ('quantum_params', 'post_w', 'post_b')}
    del _L0_txt_all

    def _L0_attn_setup():
        import jax, jax.numpy as jnp
        import numpy as np

        def _reference_tuple_inner(x, state, W_in, conv_w, conv_b, W_x, W_dt, b_dt, A_log, D, W_out):
            b, l, d = x.shape
            n = A_log.shape[1]
            dc = conv_w.shape[1]
            xz = x @ W_in
            x_ssm, z = jnp.split(xz, 2, axis=-1)
            xp = jnp.pad(x_ssm, ((0, 0), (dc - 1, 0), (0, 0)))
            x_conv = conv_b
            for k in range(dc):
                x_conv = x_conv + xp[:, k:k + l, :] * conv_w[:, k]
            x_ssm = jax.nn.silu(x_conv)
            A = -jnp.exp(A_log)
            dt = jax.nn.softplus(x_ssm @ W_dt + b_dt)
            B_seq, C_seq = jnp.split(x_ssm @ W_x, 2, axis=-1)

            def step(s, inp):
                x_t, B_t, C_t, dt_t = inp
                dA = jnp.exp(dt_t[:, :, None] * A)
                s = s * dA + B_t[:, None, :] * x_t[:, :, None]
                y = jnp.einsum('bdn,bn->bd', s, C_t) + D * x_t
                return (s, y)
            s0 = jnp.zeros((b, d, n), x.dtype)
            _, ys = jax.lax.scan(step, s0, (x_ssm.transpose(1, 0, 2), B_seq.transpose(1, 0, 2), C_seq.transpose(1, 0, 2), dt.transpose(1, 0, 2)))
            y = ys.transpose(1, 0, 2)
            y = y * jax.nn.silu(z)
            out = y @ W_out
            return (out, state)
        key = jax.random.key(seed)
        ks = jax.random.split(key, 10)
        b, l, d, n, dc = (4, 1024, 192, 16, 4)
        w = lambda k, shape, s: jax.random.normal(k, shape, jnp.float32) * s
        return {'x': w(ks[0], (b, l, d), 1.0), 'state': jnp.zeros((b, d, n), jnp.float32), 'W_in': w(ks[1], (d, 2 * d), 0.02), 'conv_w': w(ks[2], (d, dc), 0.1), 'conv_b': w(ks[3], (d,), 0.02), 'W_x': w(ks[4], (d, 2 * n), 0.02), 'W_dt': w(ks[5], (d, d), 0.02), 'b_dt': w(ks[6], (d,), 0.02), 'A_log': w(ks[7], (d, n), 0.1), 'D': jnp.ones((d,), jnp.float32), 'W_out': w(ks[8], (d, d), 0.02)}
    _L0_attn_all = _L0_attn_setup()
    _L0_attn_in = {k: v for k, v in _L0_attn_all.items() if k in ('state', 'W_in', 'conv_w', 'conv_b', 'W_x', 'W_dt', 'b_dt', 'A_log', 'D', 'W_out')}
    del _L0_attn_all

    def _L0_ffn_setup():
        import jax, jax.numpy as jnp
        import numpy as np
        NUM_EXPERTS = 8
        TOP_K = 2
        CAPACITY_FACTOR = 1.25
        MAX_GROUP_SIZE = 1024
        MIN_EXPERT_CAPACITY = 4

        def _moe_forward(x, w_router, wi, wo):
            B, T, D = x.shape
            E = NUM_EXPERTS
            num_tokens = B * T
            G = max(num_tokens // MAX_GROUP_SIZE, E)
            while num_tokens % G != 0 or G % E != 0:
                G += 1
            S = num_tokens // G
            C = max(int(TOP_K * CAPACITY_FACTOR * S / E), MIN_EXPERT_CAPACITY)
            xg = x.reshape(G, S, D)
            logits = jnp.einsum('gsd,de->gse', xg.astype(jnp.float32), w_router.astype(jnp.float32))
            probs = jax.nn.softmax(logits, axis=-1)
            gate, idx = jax.lax.top_k(probs, TOP_K)
            idx_kf = jnp.swapaxes(idx, 1, 2).reshape(G, TOP_K * S)
            mask = jax.nn.one_hot(idx_kf, E, dtype=jnp.int32)
            prio = jnp.cumsum(mask, axis=1) * mask - 1
            prio = jnp.swapaxes(prio.reshape(G, TOP_K, S, E), 1, 2)
            prio_se = prio.max(axis=2)
            gate_se = jnp.einsum('gsk,gske->gse', gate, jax.nn.one_hot(idx, E, dtype=gate.dtype))
            dispatch = jax.nn.one_hot(prio_se, C, dtype=x.dtype)
            combine = dispatch * gate_se[..., None].astype(x.dtype)
            expert_in = jnp.einsum('gsec,gsd->egcd', dispatch, xg)
            h = jax.nn.relu(jnp.einsum('egcd,edf->egcf', expert_in, wi))
            expert_out = jnp.einsum('egcf,efd->egcd', h, wo)
            out = jnp.einsum('gsec,egcd->gsd', combine, expert_out)
            return out.reshape(B, T, D)
        key = jax.random.key(seed)
        k1, k2, k3, k4 = jax.random.split(key, 4)
        B, T, D, F = (8, 256, 192, 768)
        x = jax.random.normal(k1, (B, T, D), jnp.float32)
        w_router = jax.random.normal(k2, (D, NUM_EXPERTS), jnp.float32) * D ** (-0.5)
        wi = jax.random.normal(k3, (NUM_EXPERTS, D, F), jnp.float32) * D ** (-0.5)
        wo = jax.random.normal(k4, (NUM_EXPERTS, F, D), jnp.float32) * F ** (-0.5)
        return {'x': x, 'w_router': w_router, 'wi': wi, 'wo': wo}
    _L0_ffn_all = _L0_ffn_setup()
    _L0_ffn_in = {k: v for k, v in _L0_ffn_all.items() if k in ('w_router', 'wi', 'wo')}
    del _L0_ffn_all

    def _L1_attn_setup():
        import jax, jax.numpy as jnp
        import numpy as np
        EMBED_DIM = 192
        SEQ_LEN = 256
        BATCH = 16
        ALPHA = 0.99
        key = jax.random.key(seed)
        k_x, k_w, k_b = jax.random.split(key, 3)
        d = EMBED_DIM
        x = jax.random.normal(k_x, (BATCH, SEQ_LEN, d), dtype=jnp.float32)
        lim = 1.0 / np.sqrt(d)
        W_qkv = jax.random.uniform(k_w, (3 * d, d), dtype=jnp.float32, minval=-lim, maxval=lim)
        b_qkv = jax.random.uniform(k_b, (3 * d,), dtype=jnp.float32, minval=-lim, maxval=lim)
        return {'x': x, 'W_qkv': W_qkv, 'b_qkv': b_qkv}
    _L1_attn_all = _L1_attn_setup()
    _L1_attn_in = {k: v for k, v in _L1_attn_all.items() if k in ('W_qkv', 'b_qkv')}
    del _L1_attn_all

    def _L1_ffn_setup():
        import jax, jax.numpy as jnp
        import numpy as np
        GT0 = [[0, 1, 0, 0, 1, 0], [0, 1, 0, 0, 0, 1], [0, 0, 1, 0, 1, 0], [0, 0, 1, 0, 0, 1], [0, 0, 0, 1, 1, 0], [0, 0, 0, 1, 0, 1]]
        NCLS = 6
        K = 1

        def _expert_pairs():
            pairs = []
            for i in range(NCLS):
                p = [(j - 1, k - 1) for j in range(1, 6) for k in range(1, 6) if j != k and GT0[i][j] == 1 and (GT0[i][k] == 1)]
                pairs.append(p)
            return pairs
        PAIRS = _expert_pairs()
        B, P, D, H = (64, 64, 192, 768)

        def _gelu(t):
            return jax.nn.gelu(t, approximate=False)
        key = jax.random.key(seed)
        ks = jax.random.split(key, 8)
        s = 0.02
        x = jax.random.normal(ks[0], (B, NCLS + P, D), dtype=jnp.float32)
        mids = jax.random.randint(ks[1], (B,), 0, 6)
        moe0_W1 = jax.random.normal(ks[2], (D, H), dtype=jnp.float32) * s
        moe0_b1 = jnp.zeros((H,), jnp.float32)
        moe0_W2 = jax.random.normal(ks[3], (H, D), dtype=jnp.float32) * s
        moe0_b2 = jnp.zeros((D,), jnp.float32)
        A1_W = jax.random.normal(ks[4], (5, D, H), dtype=jnp.float32) * s
        A1_b = jnp.zeros((5, H), jnp.float32)
        A2_W = jax.random.normal(ks[5], (5, H, D), dtype=jnp.float32) * s
        A2_b = jnp.zeros((5, D), jnp.float32)
        G_W = jax.random.normal(ks[6], (NCLS, D, 2), dtype=jnp.float32) * s
        return {'x': x, 'moe0_W1': moe0_W1, 'moe0_b1': moe0_b1, 'moe0_W2': moe0_W2, 'moe0_b2': moe0_b2, 'A1_W': A1_W, 'A1_b': A1_b, 'A2_W': A2_W, 'A2_b': A2_b, 'G_W': G_W, 'mids': mids}
    _L1_ffn_all = _L1_ffn_setup()
    _L1_ffn_in = {k: v for k, v in _L1_ffn_all.items() if k in ('moe0_W1', 'moe0_b1', 'moe0_W2', 'moe0_b2', 'A1_W', 'A1_b', 'A2_W', 'A2_b', 'G_W', 'mids')}
    del _L1_ffn_all
    return {'x': x, 'x_txt': x_txt, 'L0_tok_stem_w': _L0_tok_in['stem_w'], 'L0_tok_stem_b': _L0_tok_in['stem_b'], 'L0_tok_bn1_g': _L0_tok_in['bn1_g'], 'L0_tok_bn1_b': _L0_tok_in['bn1_b'], 'L0_tok_bn1_m': _L0_tok_in['bn1_m'], 'L0_tok_bn1_v': _L0_tok_in['bn1_v'], 'L0_tok_off_w': _L0_tok_in['off_w'], 'L0_tok_off_b': _L0_tok_in['off_b'], 'L0_tok_dcn_w': _L0_tok_in['dcn_w'], 'L0_tok_dcn_b': _L0_tok_in['dcn_b'], 'L0_tok_bn2_g': _L0_tok_in['bn2_g'], 'L0_tok_bn2_b': _L0_tok_in['bn2_b'], 'L0_tok_bn2_m': _L0_tok_in['bn2_m'], 'L0_tok_bn2_v': _L0_tok_in['bn2_v'], 'L0_txt_quantum_params': _L0_txt_in['quantum_params'], 'L0_txt_post_w': _L0_txt_in['post_w'], 'L0_txt_post_b': _L0_txt_in['post_b'], 'L0_attn_state': _L0_attn_in['state'], 'L0_attn_W_in': _L0_attn_in['W_in'], 'L0_attn_conv_w': _L0_attn_in['conv_w'], 'L0_attn_conv_b': _L0_attn_in['conv_b'], 'L0_attn_W_x': _L0_attn_in['W_x'], 'L0_attn_W_dt': _L0_attn_in['W_dt'], 'L0_attn_b_dt': _L0_attn_in['b_dt'], 'L0_attn_A_log': _L0_attn_in['A_log'], 'L0_attn_D': _L0_attn_in['D'], 'L0_attn_W_out': _L0_attn_in['W_out'], 'L0_ffn_w_router': _L0_ffn_in['w_router'], 'L0_ffn_wi': _L0_ffn_in['wi'], 'L0_ffn_wo': _L0_ffn_in['wo'], 'L1_attn_W_qkv': _L1_attn_in['W_qkv'], 'L1_attn_b_qkv': _L1_attn_in['b_qkv'], 'L1_ffn_moe0_W1': _L1_ffn_in['moe0_W1'], 'L1_ffn_moe0_b1': _L1_ffn_in['moe0_b1'], 'L1_ffn_moe0_W2': _L1_ffn_in['moe0_W2'], 'L1_ffn_moe0_b2': _L1_ffn_in['moe0_b2'], 'L1_ffn_A1_W': _L1_ffn_in['A1_W'], 'L1_ffn_A1_b': _L1_ffn_in['A1_b'], 'L1_ffn_A2_W': _L1_ffn_in['A2_W'], 'L1_ffn_A2_b': _L1_ffn_in['A2_b'], 'L1_ffn_G_W': _L1_ffn_in['G_W'], 'L1_ffn_mids': _L1_ffn_in['mids']}

def reference(x, x_txt, L0_tok_stem_w, L0_tok_stem_b, L0_tok_bn1_g, L0_tok_bn1_b, L0_tok_bn1_m, L0_tok_bn1_v, L0_tok_off_w, L0_tok_off_b, L0_tok_dcn_w, L0_tok_dcn_b, L0_tok_bn2_g, L0_tok_bn2_b, L0_tok_bn2_m, L0_tok_bn2_v, L0_txt_quantum_params, L0_txt_post_w, L0_txt_post_b, L0_attn_state, L0_attn_W_in, L0_attn_conv_w, L0_attn_conv_b, L0_attn_W_x, L0_attn_W_dt, L0_attn_b_dt, L0_attn_A_log, L0_attn_D, L0_attn_W_out, L0_ffn_w_router, L0_ffn_wi, L0_ffn_wo, L1_attn_W_qkv, L1_attn_b_qkv, L1_ffn_moe0_W1, L1_ffn_moe0_b1, L1_ffn_moe0_W2, L1_ffn_moe0_b2, L1_ffn_A1_W, L1_ffn_A1_b, L1_ffn_A2_W, L1_ffn_A2_b, L1_ffn_G_W, L1_ffn_mids):
    import jax
    import jax.numpy as jnp

    def _L0_tok_ref(x, stem_w, stem_b, bn1_g, bn1_b, bn1_m, bn1_v, off_w, off_b, dcn_w, dcn_b, bn2_g, bn2_b, bn2_m, bn2_v):
        import jax, jax.numpy as jnp
        import numpy as np
        K = 4
        STRIDE = 4
        EPS = 1e-05
        SLOPE = 0.01

        def conv2d(x, w, b, stride):
            out = jax.lax.conv_general_dilated(x, w, (stride, stride), 'VALID', dimension_numbers=('NCHW', 'OIHW', 'NCHW'))
            return out + b[None, :, None, None]

        def batchnorm(x, g, b, m, v):
            inv = g / jnp.sqrt(v + EPS)
            return x * inv[None, :, None, None] + (b - m * inv)[None, :, None, None]

        def leaky_relu(x):
            return jnp.where(x >= 0, x, SLOPE * x)

        def deform_conv(x, offset, w, b):
            B, C, H, W = x.shape
            Ho, Wo = (offset.shape[2], offset.shape[3])
            KK = K * K
            off = offset.reshape(B, KK, 2, Ho, Wo)
            kh = jnp.repeat(jnp.arange(K), K).astype(x.dtype)
            kw = jnp.tile(jnp.arange(K), K).astype(x.dtype)
            base_y = (jnp.arange(Ho) * STRIDE).astype(x.dtype)
            base_x = (jnp.arange(Wo) * STRIDE).astype(x.dtype)
            py = base_y[None, None, :, None] + kh[None, :, None, None] + off[:, :, 0]
            px = base_x[None, None, None, :] + kw[None, :, None, None] + off[:, :, 1]
            y0 = jnp.floor(py)
            x0 = jnp.floor(px)
            wy = py - y0
            wx = px - x0

            def corner(yc, xc):
                yi = yc.astype(jnp.int32)
                xi = xc.astype(jnp.int32)
                valid = (yi >= 0) & (yi < H) & (xi >= 0) & (xi < W)
                yi = jnp.clip(yi, 0, H - 1)
                xi = jnp.clip(xi, 0, W - 1)
                v = jax.vmap(lambda img, a, c: img[:, a, c])(x, yi, xi)
                return v * valid[:, None].astype(x.dtype)
            v00 = corner(y0, x0)
            v01 = corner(y0, x0 + 1)
            v10 = corner(y0 + 1, x0)
            v11 = corner(y0 + 1, x0 + 1)
            wy_ = wy[:, None]
            wx_ = wx[:, None]
            sampled = v00 * (1 - wy_) * (1 - wx_) + v01 * (1 - wy_) * wx_ + v10 * wy_ * (1 - wx_) + v11 * wy_ * wx_
            out = jnp.einsum('bckhw,ock->bohw', sampled, w.reshape(w.shape[0], C, KK))
            return out + b[None, :, None, None]
        h = conv2d(x, stem_w, stem_b, 4)
        h = leaky_relu(batchnorm(h, bn1_g, bn1_b, bn1_m, bn1_v))
        offset = conv2d(h, off_w, off_b, 4)
        h = deform_conv(h, offset, dcn_w, dcn_b)
        h = leaky_relu(batchnorm(h, bn2_g, bn2_b, bn2_m, bn2_v))
        B, C, Ho, Wo = h.shape
        return h.reshape(B, C, Ho * Wo).transpose(0, 2, 1)

    def _L0_txt_ref(token_ids, quantum_params, post_w, post_b):
        import jax, jax.numpy as jnp
        import numpy as np
        N_QUBITS = 6
        N_LAYERS = 3
        DIM = 1 << N_QUBITS
        VOCAB = 8000
        EMBED = 192
        B, S = (16, 1024)

        def _cnot_perm(control, target):
            idx = np.arange(DIM)
            cbit = idx >> N_QUBITS - 1 - control & 1
            flipped = idx ^ 1 << N_QUBITS - 1 - target
            return np.where(cbit == 1, flipped, idx)
        _idx = np.arange(DIM)
        Z_SIGNS = np.stack([1.0 - 2.0 * (_idx >> N_QUBITS - 1 - q & 1) for q in range(N_QUBITS)], axis=1).astype(np.float32)

        def _apply_ry(state, theta, q):
            T = state.shape[0]
            left, right = (1 << q, 1 << N_QUBITS - 1 - q)
            s = state.reshape(T, left, 2, right)
            c = jnp.cos(theta * 0.5)[:, None, None]
            sn = jnp.sin(theta * 0.5)[:, None, None]
            a0, a1 = (s[:, :, 0, :], s[:, :, 1, :])
            out = jnp.stack([c * a0 - sn * a1, sn * a0 + c * a1], axis=2)
            return out.reshape(T, DIM)

        def _apply_rz(state, theta, q):
            T = state.shape[0]
            left, right = (1 << q, 1 << N_QUBITS - 1 - q)
            s = state.reshape(T, left, 2, right)
            ph = jnp.exp(1j * (theta * 0.5)).astype(state.dtype)[:, None, None]
            out = jnp.stack([jnp.conj(ph) * s[:, :, 0, :], ph * s[:, :, 1, :]], axis=2)
            return out.reshape(T, DIM)

        def _circuit_expvals(params):
            T = params.shape[0]
            state = jnp.zeros((T, DIM), dtype=jnp.complex64).at[:, 0].set(1.0)
            for layer in range(N_LAYERS):
                for q in range(N_QUBITS):
                    state = _apply_ry(state, params[:, layer, q, 0], q)
                    state = _apply_rz(state, params[:, layer, q, 1], q)
                if layer < N_LAYERS - 1:
                    for q in range(N_QUBITS - 1):
                        state = state[:, _cnot_perm(q, q + 1)]
                    if N_QUBITS > 2:
                        state = state[:, _cnot_perm(N_QUBITS - 1, 0)]
            probs = state.real ** 2 + state.imag ** 2
            return probs @ jnp.asarray(Z_SIGNS)
        b, s = token_ids.shape
        params = quantum_params[token_ids.reshape(-1)]
        ev = _circuit_expvals(params)
        emb = ev @ post_w.T + post_b
        return emb.reshape(b, s, -1)

    def _L0_attn_ref(x, state, W_in, conv_w, conv_b, W_x, W_dt, b_dt, A_log, D, W_out):
        import jax, jax.numpy as jnp
        import numpy as np

        def _reference_tuple_inner(x, state, W_in, conv_w, conv_b, W_x, W_dt, b_dt, A_log, D, W_out):
            b, l, d = x.shape
            n = A_log.shape[1]
            dc = conv_w.shape[1]
            xz = x @ W_in
            x_ssm, z = jnp.split(xz, 2, axis=-1)
            xp = jnp.pad(x_ssm, ((0, 0), (dc - 1, 0), (0, 0)))
            x_conv = conv_b
            for k in range(dc):
                x_conv = x_conv + xp[:, k:k + l, :] * conv_w[:, k]
            x_ssm = jax.nn.silu(x_conv)
            A = -jnp.exp(A_log)
            dt = jax.nn.softplus(x_ssm @ W_dt + b_dt)
            B_seq, C_seq = jnp.split(x_ssm @ W_x, 2, axis=-1)

            def step(s, inp):
                x_t, B_t, C_t, dt_t = inp
                dA = jnp.exp(dt_t[:, :, None] * A)
                s = s * dA + B_t[:, None, :] * x_t[:, :, None]
                y = jnp.einsum('bdn,bn->bd', s, C_t) + D * x_t
                return (s, y)
            s0 = jnp.zeros((b, d, n), x.dtype)
            _, ys = jax.lax.scan(step, s0, (x_ssm.transpose(1, 0, 2), B_seq.transpose(1, 0, 2), C_seq.transpose(1, 0, 2), dt.transpose(1, 0, 2)))
            y = ys.transpose(1, 0, 2)
            y = y * jax.nn.silu(z)
            out = y @ W_out
            return (out, state)
        return _reference_tuple_inner(x, state, W_in, conv_w, conv_b, W_x, W_dt, b_dt, A_log, D, W_out)[0]

    def _L0_ffn_ref(x, w_router, wi, wo):
        import jax, jax.numpy as jnp
        import numpy as np
        NUM_EXPERTS = 8
        TOP_K = 2
        CAPACITY_FACTOR = 1.25
        MAX_GROUP_SIZE = 1024
        MIN_EXPERT_CAPACITY = 4

        def _moe_forward(x, w_router, wi, wo):
            B, T, D = x.shape
            E = NUM_EXPERTS
            num_tokens = B * T
            G = max(num_tokens // MAX_GROUP_SIZE, E)
            while num_tokens % G != 0 or G % E != 0:
                G += 1
            S = num_tokens // G
            C = max(int(TOP_K * CAPACITY_FACTOR * S / E), MIN_EXPERT_CAPACITY)
            xg = x.reshape(G, S, D)
            logits = jnp.einsum('gsd,de->gse', xg.astype(jnp.float32), w_router.astype(jnp.float32))
            probs = jax.nn.softmax(logits, axis=-1)
            gate, idx = jax.lax.top_k(probs, TOP_K)
            idx_kf = jnp.swapaxes(idx, 1, 2).reshape(G, TOP_K * S)
            mask = jax.nn.one_hot(idx_kf, E, dtype=jnp.int32)
            prio = jnp.cumsum(mask, axis=1) * mask - 1
            prio = jnp.swapaxes(prio.reshape(G, TOP_K, S, E), 1, 2)
            prio_se = prio.max(axis=2)
            gate_se = jnp.einsum('gsk,gske->gse', gate, jax.nn.one_hot(idx, E, dtype=gate.dtype))
            dispatch = jax.nn.one_hot(prio_se, C, dtype=x.dtype)
            combine = dispatch * gate_se[..., None].astype(x.dtype)
            expert_in = jnp.einsum('gsec,gsd->egcd', dispatch, xg)
            h = jax.nn.relu(jnp.einsum('egcd,edf->egcf', expert_in, wi))
            expert_out = jnp.einsum('egcf,efd->egcd', h, wo)
            out = jnp.einsum('gsec,egcd->gsd', combine, expert_out)
            return out.reshape(B, T, D)
        return _moe_forward(x, w_router, wi, wo)

    def _L1_attn_ref(x, W_qkv, b_qkv):
        import jax, jax.numpy as jnp
        import numpy as np
        EMBED_DIM = 192
        SEQ_LEN = 256
        BATCH = 16
        ALPHA = 0.99
        bs, sl, d = x.shape
        qkv = x @ W_qkv.T + b_qkv
        q, k, v = jnp.split(qkv, 3, axis=-1)
        idx = jnp.arange(sl)
        diff = idx[:, None] - idx[None, :]
        M = jnp.where(diff >= 0, jnp.float32(ALPHA) ** diff.astype(jnp.float32), 0.0)
        dim_sqrt = jnp.asarray(d, jnp.float32) ** 0.5
        scores = jnp.einsum('bsd,btd->bst', q, k) / dim_sqrt * M
        out = jnp.einsum('bst,btd->bsd', scores, v)
        return out

    def _L1_ffn_ref(x, moe0_W1, moe0_b1, moe0_W2, moe0_b2, A1_W, A1_b, A2_W, A2_b, G_W, mids):
        import jax, jax.numpy as jnp
        import numpy as np
        GT0 = [[0, 1, 0, 0, 1, 0], [0, 1, 0, 0, 0, 1], [0, 0, 1, 0, 1, 0], [0, 0, 1, 0, 0, 1], [0, 0, 0, 1, 1, 0], [0, 0, 0, 1, 0, 1]]
        NCLS = 6
        K = 1

        def _expert_pairs():
            pairs = []
            for i in range(NCLS):
                p = [(j - 1, k - 1) for j in range(1, 6) for k in range(1, 6) if j != k and GT0[i][j] == 1 and (GT0[i][k] == 1)]
                pairs.append(p)
            return pairs
        PAIRS = _expert_pairs()
        B, P, D, H = (64, 64, 192, 768)

        def _gelu(t):
            return jax.nn.gelu(t, approximate=False)
        cls_tokens = x[:, :NCLS]
        patch_tokens = x[:, NCLS:]
        patch_out = _gelu(patch_tokens @ moe0_W1 + moe0_b1) @ moe0_W2 + moe0_b2
        cls_outs = []
        for i in range(NCLS):
            tok = cls_tokens[:, i]
            eouts = [_gelu(tok @ A1_W[a] + A1_b[a]) @ A2_W[c] + A2_b[c] for a, c in PAIRS[i]]
            out = jnp.stack(eouts, axis=-1)
            gate = jax.nn.softmax(tok @ G_W[i], axis=-1)
            thr = jnp.sort(gate, axis=-1)[..., -(K + 1)]
            mask = (gate > thr[..., None]).astype(gate.dtype)
            g = gate * mask
            g = g / jnp.clip(jnp.sum(g, axis=-1, keepdims=True), 1e-06)
            cls_outs.append(jnp.sum(out * g[:, None, :], axis=-1))
        cls_out = jnp.stack(cls_outs, axis=1)
        return jnp.concatenate([cls_out, patch_out], axis=1)
    h = _L0_tok_ref(x, L0_tok_stem_w, L0_tok_stem_b, L0_tok_bn1_g, L0_tok_bn1_b, L0_tok_bn1_m, L0_tok_bn1_v, L0_tok_off_w, L0_tok_off_b, L0_tok_dcn_w, L0_tok_dcn_b, L0_tok_bn2_g, L0_tok_bn2_b, L0_tok_bn2_m, L0_tok_bn2_v)
    h = jnp.concatenate([h, _L0_txt_ref(x_txt, L0_txt_quantum_params, L0_txt_post_w, L0_txt_post_b)], axis=1)
    h = h + _L0_attn_ref(_layernorm(h, axis=-1), L0_attn_state, L0_attn_W_in, L0_attn_conv_w, L0_attn_conv_b, L0_attn_W_x, L0_attn_W_dt, L0_attn_b_dt, L0_attn_A_log, L0_attn_D, L0_attn_W_out)
    h = h + _L0_ffn_ref(_layernorm(h, axis=-1), L0_ffn_w_router, L0_ffn_wi, L0_ffn_wo)
    h = h + _L1_attn_ref(_layernorm(h, axis=-1), L1_attn_W_qkv, L1_attn_b_qkv)
    h = h + _L1_ffn_ref(_layernorm(h, axis=-1), L1_ffn_moe0_W1, L1_ffn_moe0_b1, L1_ffn_moe0_W2, L1_ffn_moe0_b2, L1_ffn_A1_W, L1_ffn_A1_b, L1_ffn_A2_W, L1_ffn_A2_b, L1_ffn_G_W, L1_ffn_mids)
    return h

_drawn_inputs = setup_inputs


def setup_inputs(seed=0):
    import zlib

    import numpy as np

    out = dict(_drawn_inputs(seed))
    spreads = {'L0_attn_state': (0.0, 0.1),
     'L0_attn_D': (1.0, 0.6),
     'L1_ffn_moe0_b1': (0.0, 0.8),
     'L1_ffn_moe0_b2': (0.0, 1.264),
     'L1_ffn_A1_b': (0.0, 2.0),
     'L1_ffn_A2_b': (0.0, 2.0)}
    factors = {'L0_txt_post_b': 4.222,
     'L0_attn_W_in': 4.109,
     'L0_attn_conv_w': 4.372,
     'L0_attn_conv_b': 8.0,
     'L0_attn_W_x': 8.0,
     'L0_attn_W_dt': 8.0,
     'L0_attn_b_dt': 8.0,
     'L0_attn_A_log': 8.0,
     'L0_attn_W_out': 2.897,
     'L1_ffn_moe0_W1': 3.464,
     'L1_ffn_moe0_W2': 3.299,
     'L1_ffn_A1_W': 8.0,
     'L1_ffn_A2_W': 8.0,
     'L1_ffn_G_W': 8.0}
    for name, (base, spread) in spreads.items():
        noise = np.random.default_rng([zlib.crc32(name.encode()), seed]).standard_normal(out[name].shape)
        drawn = base * np.exp(spread * noise) if base else spread * noise
        out[name] = jnp.asarray(drawn.astype(out[name].dtype))
    for name, factor in factors.items():
        out[name] = (out[name] * factor).astype(out[name].dtype)
    return out
```

```python
from contextlib import ExitStack, contextmanager

import numpy as np

import concourse.bass as bass
from concourse import mybir

ALU = mybir.AluOpType
ACT = mybir.ActivationFunctionType
AX = mybir.AxisListType
F32 = mybir.dt.float32
BF16 = mybir.dt.bfloat16
I32 = mybir.dt.int32

B = 16
D = 192
DA, DR = 128, 64
NP_TOK = 196
NT_TXT = 512
L = NP_TOK + NT_TXT
TC = 118
NC = L // TC
HL = L // 2
F = 768
FC = F // 128
EPS = 1e-5

CIN, COUT = 96, 192
STEM_K = 96
IMG = 56
ENT = 58
PADW = 59
TAPS = 16
POS = 98
SLOTS = 4
ST = 8

NQ = 6
TCOL = B * NT_TXT // 128

NS = 16

E = 8
CAP = int(2 * 1.25 * L / E)
SLOT = E * CAP
TRASH = 2 * L
XROWS = 104
XCH = SLOT // XROWS

NCLS = 6
NA = 5
PAIRS = [((0, 3), (3, 0)), ((0, 4), (4, 0)), ((1, 3), (3, 1)), ((1, 4), (4, 1)), ((2, 3), (3, 2)), ((2, 4), (4, 2))]

@contextmanager
def semaphores(nc):
    held = []

    def allocate(name):
        held.append(nc.alloc_semaphore(name=name))
        return held[-1]

    yield allocate
    nc.clear_and_free_semaphores(held)
    nc.all_engine_barrier()


def wait(eng, sem, value):
    if isinstance(value, int) and value <= 0:
        return
    eng.wait_ge(sem, value)


def wait_alone(eng, sem, value, passed):
    if isinstance(value, int) and value <= 0:
        return
    eng.wait_ge(sem, value)
    eng.sem_inc(passed, 1)


def pipeline(eng, total, turn, parts, peel=1):
    def units(base, first):
        for j in range(turn):
            for lag, f in parts:
                if j >= lag or not first:
                    f(base + (j - lag), (j - lag) % turn)

    assert total % turn == 0 and total > peel * turn and all(lag <= turn for lag, _ in parts)
    for i in range(peel):
        units(i * turn, i == 0)
    with eng.Fori(peel, total // turn) as i:
        units(i * turn, False)
    for j in range(max(lag for lag, _ in parts)):
        for lag, f in parts:
            if j < lag:
                f(total + j - lag, (j - lag) % turn)


def statistics(dve, h, stat, mv):
    for c in range(NC):
        dve.bn_stats(stat[:, c, :], h[:, c, :])
    dve.drain()
    for c in range(NC):
        dve.bn_aggr(mv[:, c, :], stat[:, c, :])
    dve.drain()
    return dve.tensor_scalar(mv[:, :, 1], mv[:, :, 1], EPS, None, ALU.add)


def tokenizer_fold(nc, d, W):
    with ExitStack() as ctx:
        def sb(name, shape, dt=F32):
            return ctx.enter_context(nc.sbuf_tensor(name + "_sb", shape, dt))

        bn1 = sb("bn1", [1, 5, CIN])
        bn2 = sb("bn2", [1, 5, COUT])
        ones = sb("fold_ones", [1, 128])
        inv_ps = ctx.enter_context(nc.psum_tensor("inv_ps", [128, COUT + CIN], F32))
        count = ctx.enter_context(semaphores(nc))
        loaded = count("fold_loaded")
        var_ready = count("fold_var")
        root_ready = count("fold_root")
        inv_ready = count("fold_inv")
        spread = count("fold_spread")
        block = ctx.enter_context(nc.Block())

        @block.sync
        def _(sp):
            sp.dma_start(bn1[:, :, :], d["bn1"]).then_inc(loaded, 16)
            sp.dma_start(bn2[:, :, :], d["bn2"]).then_inc(loaded, 16)
            sp.dma_start(W["stem_w"][:, :], d["stem_w"]).then_inc(loaded, 16)
            sp.dma_start(W["dcn_w"][:, :, :], d["dcn_w"]).then_inc(loaded, 16)
            sp.dma_start(W["off_w"][:, :, :], d["off_w"]).then_inc(loaded, 16)
            sp.dma_start(W["off_b"][:, :], d["off_b"]).then_inc(loaded, 16)
            sp.dma_start(W["grid"][:, :, :, :], d["grid"]).then_inc(loaded, 16)
            sp.dma_start(W["ident"][:, :], d["ident"]).then_inc(loaded, 16)
            sp.dma_start(W["patches"][:, :, :], d["patch_frame"]).then_inc(loaded, 16)

        @block.scalar
        def _(act):
            act.wait_ge(var_ready, 1)
            act.activation(bn1[:, 4, :], bn1[:, 4, :], ACT.Sqrt)
            act.activation(bn2[:, 4, :], bn2[:, 4, :], ACT.Sqrt).then_inc(root_ready, 1)

        @block.vector
        def _(dve):
            dve.memset(ones[:, :], 1.0)
            dve.memset(W["ones"][:, :], 1.0)
            dve.memset(W["pix"][:, :, :], 0.0)
            dve.wait_ge(loaded, 16 * 9)
            dve.tensor_scalar(bn1[:, 4, :], bn1[:, 4, :], EPS, None, ALU.add)
            dve.tensor_scalar(bn2[:, 4, :], bn2[:, 4, :], EPS, None, ALU.add).then_inc(var_ready, 1)
            dve.wait_ge(root_ready, 1)
            for bn in (bn1, bn2):
                dve.reciprocal(bn[:, 4, :], bn[:, 4, :])
            dve.drain()
            for bn in (bn1, bn2):
                dve.tensor_tensor(bn[:, 1, :], bn[:, 1, :], bn[:, 4, :], ALU.mult)
            dve.drain().then_inc(inv_ready, 1)
            for bn in (bn1, bn2):
                dve.tensor_tensor(bn[:, 3, :], bn[:, 3, :], bn[:, 1, :], ALU.mult)
                dve.tensor_tensor(bn[:, 0, :], bn[:, 0, :], bn[:, 1, :], ALU.mult)
            dve.drain()
            for bn in (bn1, bn2):
                dve.tensor_tensor(bn[:, 2, :], bn[:, 2, :], bn[:, 3, :], ALU.subtract)
            dve.drain()
            dve.tensor_tensor(W["dcn_b"][:, :], bn2[:, 0, :], bn2[:, 2, :], ALU.add)
            dve.wait_ge(spread, 1)
            dve.tensor_tensor(W["stem_w"][:, :], W["stem_w"][:, :], inv_ps[0:STEM_K, COUT:COUT + CIN], ALU.mult)
            for j in range(12):
                dve.tensor_tensor(W["dcn_w"][:, j, :], W["dcn_w"][:, j, :], inv_ps[:, 0:COUT], ALU.mult)
            dve.drain()
            dve.tensor_tensor(W["stem_w"][0:1, :], bn1[:, 0, :], bn1[:, 2, :], ALU.add)

        @block.tensor
        def _(pe):
            pe.wait_ge(inv_ready, 1)
            pe.matmul(inv_ps[:, 0:COUT], ones[:, :], bn2[:, 1, :], start=True, stop=True)
            pe.matmul(inv_ps[:, COUT:COUT + CIN], ones[:, :], bn1[:, 1, :], start=True, stop=True).then_inc(spread, 1)


def tokenizer(nc, d, keep, text):
    tables = [d["corner_table0"], d["corner_table1"]]
    tabs = [t.rearrange("(y x) s c -> y x s c", y=ENT) for t in tables]

    patches_d = d["patches"]
    with ExitStack() as ctx:
        def sb(name, shape, dt=F32):
            return ctx.enter_context(nc.sbuf_tensor(name + "_sb", shape, dt))

        def ps(name, shape):
            return ctx.enter_context(nc.psum_tensor(name, shape, F32))

        count = ctx.enter_context(semaphores(nc))

        def sem(name):
            return count(name)

        def kept_sem(name):
            return keep.enter_context(nc.semaphore(name))

        W = {
            "stem_w": sb("stem_w", [STEM_K, CIN]),
            "dcn_w": sb("dcn_w", [128, 12, COUT]),
            "dcn_b": sb("dcn_b", [1, COUT]),
            "off_w": sb("off_w", [CIN, TAPS, 32]),
            "off_b": sb("off_b", [1, 32]),
            "grid": sb("grid", [POS, 2, 2, TAPS]),
            "ident": sb("ident", [128, 128]),
            "ones": sb("ones", [1, 128]),
            "patches": sb("patches", [STEM_K, 2 * ENT, PADW]),
            "pix": sb("pix", [2 * ENT, PADW, CIN]),
        }
        tokenizer_fold(nc, d, W)
        patches, pix = W["patches"], W["pix"]
        feat = sb("feat", [CIN, TAPS, NP_TOK])
        q = sb("q", [POS, 2, 2, TAPS])
        qi = sb("qi", [POS, 2, 2, TAPS], I32)
        fl = sb("fl", [POS, 2, 2, TAPS])
        up = sb("up", [POS, 2, 2, TAPS])
        lin = sb("lin", [POS, 2, TAPS])
        index = [sb(f"index{i}", [POS, 2, TAPS], I32) for i in range(2)]
        wgt = [sb(f"wgt{i}", [POS, 2, TAPS, 4]) for i in range(2)]
        corners = sb("corners", [POS, SLOTS, ST, 4 * CIN])
        sampled = [sb(f"sampled{i}", [POS, SLOTS, ST * CIN]) for i in range(2)]
        sampT = sb("sampT", [128, 12, POS])
        token = sb("token", [POS, 2, COUT])

        stem_ps = ps("stem_ps", [128, 4, 512])
        off_ps = ps("off_ps", [POS, 2, 32])
        tr_ps = ps("tr_ps", [128, 2, 512])
        tok_ps = ps("tok_ps", [POS, COUT])

        patches_in = sem("patches_in")
        patches_used = sem("patches_used")
        stem_mm = sem("stem_mm")
        stem_copied = sem("stem_copied")
        pix_ready = sem("pix_ready")
        feat_ready = sem("feat_ready")
        off_mm = sem("off_mm")
        table_out = sem("table_out")
        index_ready = sem("index_ready")
        gathered = [kept_sem(f"gathered{s}") for s in range(SLOTS)]
        sp_passed = sem("sp_passed")
        gather_opened = sem("gather_opened")
        sampled_ready = sem("sampled_ready")
        tr_mm = sem("tr_mm")
        tr_ready = sem("tr_ready")
        tok_mm = sem("tok_mm")
        tok_scaled = sem("tok_scaled")
        tok_ready = sem("tok_ready")
        tok_out = sem("tok_out")

        PG, PW = 14, 4
        FG, FT = 8, 2
        SG = PG + FG
        TG, TW = 2, 3
        block = ctx.enter_context(nc.Block())

        @block.sync
        def _(sp):
            def load(b, u):
                wait_alone(sp, patches_used, b, sp_passed)
                for first in (1, ENT):
                    sp.dma_start(patches[1:49, first:first + IMG, 1:1 + IMG], patches_d[bass.ds(b, 1)].rearrange(
                        "o k y x -> (o k) y x")).then_inc(patches_in, 16)

            def store_table(b, u):
                wait_alone(sp, pix_ready, 2 * (b + 1), sp_passed)
                for s in range(SLOTS):
                    wait_alone(sp, gathered[s], 16 * ST * (b - 1), sp_passed)
                for s in range(2):
                    for y, n in ((0, 48), (48, 10)):
                        src = pix[s * ENT + y:s * ENT + y + n, :, :]
                        src = bass.AP(src.tensor, src.offset, [list(src.ap[0]), [CIN, ENT], [1, 2 * CIN]])
                        sp.dma_start(tabs[u % 2][y:y + n, :, s, :], src).then_inc(table_out, 16)

            def store_tokens(b, u):
                for half in range(2):
                    wait_alone(sp, tok_ready, 2 * b + half + 1, sp_passed)
                    sp.dma_start(d["h0"][bass.ds(b, 1), half * POS:(half + 1) * POS, :].rearrange(
                        "o p c -> (o p) c"), token[:, half, :]).then_inc(tok_out, 16)

            sp.dma_start(text["ids"][:, :], d["token_ids"]).then_inc(text["ids_in"], 16)
            pipeline(sp, B, 4, [(0, load), (1, store_table), (3, store_tokens)])
            sp.wait_ge(tok_out, 16 * 2 * B)
            sp.wait_ge(table_out, 16 * 4 * B)

        @block.gpsimd
        def _(pool):
            def gather(b, u):
                pool.wait_ge(index_ready, b + 1)
                pool.wait_ge(table_out, 64 * (b + 1))
                for s in range(SLOTS):
                    pool.wait_ge(sampled_ready, SLOTS * b + s + 1)
                    pool.sem_inc(gather_opened, 1)
                    for t in range(ST):
                        pool.indirect_dma_start(
                            out=corners[:, s, t, :], out_offset=None,
                            in_=tables[u].rearrange("e s c -> e (s c)"),
                            in_offset=bass.IndirectOffsetOnAxis(
                                ap=index[u][:, s // 2, (s % 2) * ST + t:(s % 2) * ST + t + 1], axis=0),
                        ).then_inc(gathered[s], 16)

            def text_share(b, u):
                if isinstance(b, int) and b < 4:
                    gather_parameters(pool, d, text, b, 4, gather_opened)

            pipeline(pool, B, 2, [(0, gather), (0, text_share)], peel=2)

        @block.tensor
        def _(pe):
            def stem(b, u):
                pe.wait_ge(patches_in, 32 * (b + 1))
                for g in range(PG):
                    wait(pe, stem_copied, SG * b + g - 3)
                    for x in range(PW):
                        mm = pe.matmul(stem_ps[0:2 * ENT, (SG * u + g) % 4, x * CIN:(x + 1) * CIN],
                                       patches[:, :, 1 + g * PW + x], W["stem_w"][:, :],
                                       start=True, stop=True)
                    mm.then_inc(stem_mm, 1)
                for g in range(FG):
                    wait(pe, stem_copied, SG * b + PG + g - 3)
                    for t in range(FT):
                        ky, kx = divmod(g * FT + t, 4)
                        mm = pe.matmul(stem_ps[0:CIN, (SG * u + PG + g) % 4, t * NP_TOK:(t + 1) * NP_TOK], W["stem_w"][:, :],
                                       patches[:, 1 + ky:1 + ky + 53:4, 1 + kx:1 + kx + 53:4],
                                       start=True, stop=True)
                    mm.then_inc(stem_mm, 1)
                pe.drain().then_inc(patches_used, 1)

            def offsets(b, u):
                pe.wait_ge(feat_ready, b + 1)
                wait(pe, index_ready, b)
                for half in range(2):
                    for k in range(TAPS):
                        pe.matmul(off_ps[:, half, :], feat[:, k, half * POS:(half + 1) * POS], W["off_w"][:, k, :], start=(k == 0), stop=False)
                    mm = pe.matmul(off_ps[:, half, :], W["ones"][:, 0:POS], W["off_b"][:, :], start=False, stop=True)
                mm.then_inc(off_mm, 1)

            def deform(half):
                def f(b, u):
                    for s in (2 * half, 2 * half + 1):
                        pe.wait_ge(sampled_ready, SLOTS * (b + 1) + s + 1)
                        for g in range(TG):
                            n = (SLOTS * b + s) * TG + g
                            wait(pe, tr_ready, n)
                            for t in range(TW):
                                j = g * TW + t
                                mm = pe.transpose(tr_ps[:, g % 2, t * POS:(t + 1) * POS],
                                                  sampled[u][:, s, j * 128:(j + 1) * 128], W["ident"][0:POS, 0:POS])
                            mm.then_inc(tr_mm, 1)
                        if s % 2:
                            pe.wait_ge(tr_ready, 1 + (SLOTS * b + s + 1) * TG)
                            wait(pe, tok_ready, 2 * b + s // 2)
                            for j in range(12):
                                pe.matmul(tok_ps[:, :], sampT[:, j, :], W["dcn_w"][:, j, :], start=(j == 0), stop=False)
                            pe.matmul(tok_ps[:, :], W["ones"][:, 0:POS], W["dcn_b"][:, :],
                                      start=False, stop=True).then_inc(tok_mm, 1)
                return f

            pe.sem_inc(tok_mm, 1)

            pipeline(pe, B, 2, [(0, stem), (2, deform(0)), (0, offsets), (2, deform(1))], peel=2)

        @block.scalar
        def _(act):
            def stem(b, u):
                wait(act, table_out, 64 * b)
                for g in range(PG):
                    act.wait_ge(stem_mm, SG * b + g + 1)
                    act.activation(pix[:, 1 + g * PW:1 + (g + 1) * PW, :],
                                   stem_ps[0:2 * ENT, (SG * u + g) % 4, 0:PW * CIN].rearrange("p (x c) -> p x c", c=CIN),
                                   ACT.Copy).then_inc(stem_copied, 1)
                wait(act, off_mm, b)
                for g in range(FG):
                    act.wait_ge(stem_mm, SG * b + PG + g + 1)
                    act.activation(feat[:, g * FT:(g + 1) * FT, :],
                                   stem_ps[0:CIN, (SG * u + PG + g) % 4, 0:FT * NP_TOK].rearrange("p (t m) -> p t m", t=FT),
                                   ACT.Copy).then_inc(stem_copied, 1)

            def tokens(b, half):
                act.wait_ge(tok_mm, 1 + 2 * b + half + 1)
                wait(act, tok_out, 32 * b)
                act.activation(token[:, half, :], tok_ps[:, :], ACT.Copy, scale=0.01).then_inc(tok_scaled, 1)

            def turn(b, u):
                for s in range(SLOTS):
                    for g in range(TG):
                        act.wait_ge(tr_mm, (SLOTS * b + s) * TG + g + 1)
                        if s % 2 == 0 and g == 0:
                            act.wait_ge(tok_mm, 1 + 2 * b + s // 2)
                        j = (s % 2) * TG * TW + g * TW
                        act.activation(sampT[:, j:j + TW, :],
                                       tr_ps[:, g % 2, 0:TW * POS].rearrange("p (t m) -> p t m", t=TW),
                                       ACT.Copy).then_inc(tr_ready, 1)
                    if s % 2:
                        tokens(b, s // 2)

            act.sem_inc(tr_ready, 1)

            pipeline(act, B, 2, [(0, stem), (2, turn)], peel=2)

        @block.vector
        def _(dve):
            def stem(g):
                def f(b, u):
                    dve.wait_ge(stem_copied, SG * b + (g + 1) * PG // 2)
                    x = pix[:, 1 + g * IMG // 2:1 + (g + 1) * IMG // 2, :]
                    dve.scalar_tensor_tensor(out=x, in0=x, scalar=0.01, in1=x, op0=ALU.mult,
                                             op1=ALU.max).then_inc(pix_ready, 1)
                return f

            def stem_channels(b, u):
                dve.wait_ge(stem_copied, SG * (b + 1))
                dve.scalar_tensor_tensor(out=feat[:, :, :], in0=feat[:, :, :], scalar=0.01, in1=feat[:, :, :],
                                         op0=ALU.mult, op1=ALU.max).then_inc(feat_ready, 1)

            def points(b, u):
                dve.wait_ge(off_mm, b + 1)
                for s in range(SLOTS):
                    wait(dve, gathered[s], 16 * ST * (b - 1))
                dve.tensor_tensor(q[:, :, :, :], off_ps[:, :, :].rearrange("p h (a t) -> p h a t", a=2),
                                  W["grid"][:, :, :, :], ALU.add)
                dve.drain()
                dve.tensor_scalar(q[:, :, :, :], q[:, :, :, :], -1.0, float(IMG), ALU.max, ALU.min)
                dve.drain()
                dve.tensor_copy(qi[:, :, :, :], q[:, :, :, :])
                dve.drain()
                dve.tensor_copy(fl[:, :, :, :], qi[:, :, :, :])
                dve.drain()
                dve.tensor_tensor(up[:, :, :, :], fl[:, :, :, :], q[:, :, :, :], ALU.is_gt)
                dve.drain()
                dve.tensor_tensor(fl[:, :, :, :], fl[:, :, :, :], up[:, :, :, :], ALU.subtract)
                dve.drain()
                dve.tensor_tensor(q[:, :, :, :], q[:, :, :, :], fl[:, :, :, :], ALU.subtract)
                dve.scalar_tensor_tensor(out=lin[:, :, :], in0=fl[:, :, 0, :], scalar=float(ENT), in1=fl[:, :, 1, :],
                                         op0=ALU.mult, op1=ALU.add)
                dve.drain()
                dve.tensor_scalar(up[:, :, :, :], q[:, :, :, :], -1.0, 1.0, ALU.mult, ALU.add)
                dve.tensor_scalar(index[u][:, :, :], lin[:, :, :], float(ENT + 1), None, ALU.add)
                dve.drain()
                for k, (wy, wx) in enumerate(((up, up), (up, q), (q, up), (q, q))):
                    dve.tensor_tensor(wgt[u][:, :, :, k], wy[:, :, 0, :], wx[:, :, 1, :], ALU.mult)
                dve.drain().then_inc(index_ready, 1)

            def mix(s):
                def f(b, u):
                    dve.wait_ge(gathered[s], 16 * ST * (b + 1))
                    if s % 2 == 0:
                        wait(dve, tok_mm, 2 * (b - 1) + s // 2)
                    w = wgt[u][:, s // 2, (s % 2) * ST:(s % 2 + 1) * ST, :]
                    for k in range(4):
                        c = corners[:, s, :, k * CIN:(k + 1) * CIN]
                        dve.tensor_tensor(c, c, w[:, :, k:k + 1].to_broadcast([POS, ST, CIN]), ALU.mult)
                    dve.drain()
                    c = corners[:, s, :, :]
                    dve.tensor_tensor(c[:, :, 0:2 * CIN], c[:, :, 0:2 * CIN], c[:, :, 2 * CIN:4 * CIN], ALU.add)
                    dve.drain()
                    dve.tensor_tensor(sampled[u][:, s, :].rearrange("p (t c) -> p t c", c=CIN),
                                      c[:, :, 0:CIN], c[:, :, CIN:2 * CIN], ALU.add).then_inc(sampled_ready, 1)
                return f

            def tokens(half):
                def f(b, u):
                    dve.wait_ge(tok_scaled, 2 * b + half + 1)
                    dve.tensor_tensor(token[:, half, :], token[:, half, :], tok_ps[:, :],
                                      ALU.max).then_inc(tok_ready, 1)
                return f

            dve.sem_inc(sampled_ready, SLOTS)

            pipeline(dve, B, 2, [(0, stem(0)), (1, mix(0)), (0, stem_channels), (0, stem(1)), (1, mix(1)), (0, points),
                                 (2, tokens(0)), (1, mix(2)), (2, tokens(1)), (1, mix(3))], peel=2)


def pauli_terms():
    ring = [(q, (q + 1) % NQ) for q in range(NQ)]

    def through_ring(x, z, sign):
        x, z = list(x), list(z)
        for c, t in reversed(ring):
            if x[c] and z[t] and x[t] == z[c]:
                sign = -sign
            x[t] ^= x[c]
            z[c] ^= z[t]
        return x, z, sign

    becomes = {
        (0, 0): [(None, 0, 0)],
        (0, 1): [("zz", 0, 1), ("zx", 1, 0)],
        (1, 0): [("xx", 1, 0), ("xz", 0, 1), ("xy", 1, 1)],
    }

    def expand(x, z):
        x, z, sign = through_ring(x, z, 1)
        products = [[]]
        for q in range(NQ):
            products = [p + [f] for p in products for f in becomes[x[q], z[q]]]
        out = []
        for p in products:
            a, c, s = through_ring([f[1] for f in p], [f[2] for f in p], sign)
            out.append((tuple((f[0], (a[q], c[q])) for q, f in enumerate(p)), s))
        return out

    unit = [[int(i == q) for i in range(NQ)] for q in range(NQ)]
    zero = [0] * NQ
    return [expand(zero, u) for u in unit] + [expand(u, zero) for u in unit]


def shared_sums():
    levels = [[] for _ in range(NQ)]
    known = {}

    def build(strings, q):
        if q < 0:
            return None, strings[0][1]
        strings = sorted(strings, key=repr)
        sign = strings[0][1]
        key = (q, tuple((a, s * sign) for a, s in strings))
        if key not in known:
            groups = {}
            for a, s in strings:
                groups.setdefault(a[q], []).append((a[:q], s * sign))
            terms = []
            for (symbol, pauli), rest in groups.items():
                node, s = build(rest, q - 1)
                terms.append((symbol, pauli, node, s))
            levels[q].append(sorted(terms, key=lambda t: -t[3]))
            known[key] = len(levels[q]) - 1
        return known[key], sign

    return levels, [build(p, NQ - 1) for p in pauli_terms()]


def text_parameters(nc, keep):
    return {"ids": keep.enter_context(nc.sbuf_tensor("tx_ids", [128, TCOL], I32)),
            "params": keep.enter_context(nc.sbuf_tensor("tx_params", [128, TCOL, 6 * NQ], F32)),
            "ids_in": nc.alloc_semaphore(name="tx_ids_in"),
            "gathered": nc.alloc_semaphore(name="tx_gathered")}


def gather_parameters(pool, d, text, part, parts, passed):
    wait_alone(pool, text["ids_in"], 16, passed)
    for c in range(part * TCOL // parts, (part + 1) * TCOL // parts):
        pool.indirect_dma_start(
            out=text["params"][:, c, :], out_offset=None, in_=d["circuit"],
            in_offset=bass.IndirectOffsetOnAxis(ap=text["ids"][:, c:c + 1], axis=0)).then_inc(text["gathered"], 16)


def text_tokens(nc, d, text):
    levels, roots = shared_sums()
    most = max(len(v) for v in levels)
    most_terms = max(sum(len(t) for t in v) for v in levels)
    symbols = ["zz", "zx", "xx", "xz", "xy"]
    NA = 5 * NQ
    PI = float(np.pi)
    ROUND = 1.5 * 2.0 ** 23
    with ExitStack() as ctx:
        def sb(name, shape, dt=F32):
            return ctx.enter_context(nc.sbuf_tensor("tx_" + name, shape, dt))

        def ps(name, shape):
            return ctx.enter_context(nc.psum_tensor("tx_" + name, shape, F32))

        count = ctx.enter_context(semaphores(nc))

        def sem(name):
            return count("tx_" + name)

        zero = sb("zero", [128, 17 * D])
        ZROWS = 128 * 17
        assert B * SLOT % ZROWS == 0
        post = sb("post", [NQ + 1, D])
        ident = sb("ident_q", [128, 128])
        params, gathered = text["params"], text["gathered"]
        ang = sb("ang", [128, 2, 5, NQ, TCOL])
        turns = sb("turns", [128, 2, 5, NQ, TCOL])
        trig = sb("trig", [128, 2, 5, NQ, TCOL])
        bloch = sb("bloch", [128, 3, NQ, TCOL])
        coef = sb("coef", [128, 5, NQ, TCOL])
        both = sb("both", [128, 5, 3, NQ, TCOL])
        node = [sb(f"node{i}", [128, most, TCOL]) for i in range(2)]
        term = sb("term", [128, most_terms, TCOL])
        means = sb("means", [128, TCOL, 8])
        mean4 = [sb(f"mean4{i}", [128, 4, 8]) for i in range(2)]
        meanT = [sb(f"meanT{i}", [NQ + 1, 512]) for i in range(2)]
        emb = [sb(f"emb{i}", [128, 4, D]) for i in range(2)]
        t_ps = [ps(f"t_ps{i}", [NQ + 1, 512]) for i in range(2)]
        e_ps = [ps(f"e_ps{i}", [128, 2, 512]) for i in range(2)]

        loaded = sem("q_loaded")
        reduced = sem("q_reduced")
        trig_ready = sem("q_trig")
        mean_ready = sem("q_mean")
        turned = sem("q_turned")
        turn_ready = sem("q_turn_ready")
        emb_mm = sem("q_emb_mm")
        emb_ready = sem("q_emb_ready")
        emb_out = [sem(f"q_emb_out{i}") for i in range(2)]
        passed, zero_ready, zeroed = sem("q_passed"), sem("zero_ready"), sem("zeroed")
        block = ctx.enter_context(nc.Block())

        @block.sync
        def _(sp):
            sp.dma_start(post[:, :], d["post"]).then_inc(loaded, 16)
            sp.dma_start(ident[:, :], d["ident"]).then_inc(loaded, 16)

            def store(b, u):
                wait_alone(sp, emb_ready, b + 1, passed)
                sp.dma_start(d["h0"][bass.ds(b, 1), NP_TOK:L, :].rearrange("o (j p) c -> p (o j) c", p=128),
                             emb[u][:, :, :]).then_inc(emb_out[u], 16)

            sp.wait_ge(zero_ready, 1)
            for i in range(B * SLOT // ZROWS):
                sp.dma_start(d["xin"][i * ZROWS:(i + 1) * ZROWS, :].rearrange("(p r) c -> p (r c)", p=128),
                             zero[:, :]).then_inc(zeroed, 16)
            pipeline(sp, B, 2, [(0, store)])
            sp.wait_ge(zeroed, 16 * (B * SLOT // ZROWS))
            for u in range(2):
                sp.wait_ge(emb_out[u], 16 * B // 2)

        @block.gpsimd
        def _(pool):
            pool.memset(zero[:, :], 0.0).then_inc(zero_ready, 1)

        @block.scalar
        def _(act):
            act.wait_ge(reduced, 1)
            act.activation(trig[:, :, :, :, :], ang[:, :, :, :, :], ACT.Sin).then_inc(trig_ready, 1)

            def turn(b, u):
                act.wait_ge(turned, b + 1)
                wait(act, emb_mm, b - 1)
                act.activation(meanT[u][:, :], t_ps[u][:, :], ACT.Copy).then_inc(turn_ready, 1)

            pipeline(act, B, 2, [(0, turn)])

        @block.tensor
        def _(pe):
            pe.wait_ge(loaded, 32)

            def turn(b, u):
                pe.wait_ge(mean_ready, b + 1)
                wait(pe, turn_ready, b - 1)
                for j in range(4):
                    mm = pe.transpose(t_ps[u][:, j * 128:(j + 1) * 128], mean4[u][:, j, 0:NQ + 1], ident[:, :])
                mm.then_inc(turned, 1)

            def embed(b, u):
                pe.wait_ge(turn_ready, b + 1)
                wait(pe, emb_ready, b - 1)
                for j in range(4):
                    mm = pe.matmul(e_ps[u][:, j // 2, (j % 2) * D:(j % 2 + 1) * D], meanT[u][:, j * 128:(j + 1) * 128],
                                   post[:, :], start=True, stop=True)
                mm.then_inc(emb_mm, 1)

            pipeline(pe, B, 2, [(0, turn), (1, embed)], peel=2)

        @block.vector
        def _(dve):
            def mul(out, a, b):
                return dve.tensor_tensor(out, a, b, ALU.mult)

            dve.memset(means[:, :, NQ:8], 1.0)
            dve.wait_ge(gathered, 16 * TCOL)
            by_layer = params[:, :, :].rearrange("p c (l q k) -> p l k q c", l=3, k=2)
            for i, (layer, kind) in enumerate(((0, 0), (0, 1), (1, 0), (1, 1), (2, 0))):
                a = by_layer[:, layer, kind, :, :]
                dve.tensor_copy(ang[:, 0, i, :, :], a)
                dve.tensor_scalar(ang[:, 1, i, :, :], a, PI / 2, None, ALU.add)
            dve.drain()
            a, t = ang[:, :, :, :, :], turns[:, :, :, :, :]
            dve.tensor_scalar(t, a, 1.0 / (2.0 * PI), ROUND, ALU.mult, ALU.add)
            dve.drain()
            dve.tensor_scalar(t, t, -ROUND, -2.0 * PI, ALU.add, ALU.mult)
            dve.drain()
            dve.tensor_tensor(a, a, t, ALU.add)
            dve.drain()
            dve.tensor_scalar(a, a, float(np.float32(3.1415925)), float(np.float32(-3.1415925)), ALU.min,
                              ALU.max).then_inc(reduced, 1)
            dve.wait_ge(trig_ready, 1)
            s, c = trig[:, 0, :, :, :], trig[:, 1, :, :, :]
            mul(bloch[:, 0, :, :], s[:, 0, :, :], c[:, 1, :, :])
            dve.tensor_copy(bloch[:, 1, :, :], c[:, 0, :, :])
            mul(bloch[:, 2, :, :], s[:, 0, :, :], s[:, 1, :, :])
            dve.tensor_copy(coef[:, 0, :, :], c[:, 2, :, :])
            dve.tensor_scalar(coef[:, 1, :, :], s[:, 2, :, :], -1.0, None, ALU.mult)
            mul(coef[:, 2, :, :], c[:, 3, :, :], c[:, 2, :, :])
            mul(coef[:, 3, :, :], c[:, 3, :, :], s[:, 2, :, :])
            dve.tensor_scalar(coef[:, 4, :, :], s[:, 3, :, :], -1.0, None, ALU.mult)
            dve.drain()
            for k in range(5):
                for m in range(3):
                    mul(both[:, k, m, :, :], coef[:, k, :, :], bloch[:, m, :, :])
            component = {(1, 0): 0, (0, 1): 1, (1, 1): 2}

            def factor(q, symbol, pauli):
                if symbol is None:
                    return None if pauli == (0, 0) else bloch[:, component[pauli], q, :]
                k = symbols.index(symbol)
                return coef[:, k, q, :] if pauli == (0, 0) else both[:, k, component[pauli], q, :]

            for q, sums in enumerate(levels):
                now, before = node[q % 2], node[(q + 1) % 2]
                dve.drain()
                at, terms = 0, []
                for s_ in sums:
                    row = []
                    for symbol, pauli, below, sign in s_:
                        f = factor(q, symbol, pauli)
                        v = None if below is None else before[:, below, :]
                        if f is not None and v is not None:
                            mul(term[:, at, :], f, v)
                            row.append((term[:, at, :], sign))
                            at += 1
                        else:
                            row.append((f if f is not None else v, sign))
                    terms.append(row)
                for i in range(max(len(r) for r in terms)):
                    dve.drain()
                    for n, row in enumerate(terms):
                        if i >= len(row):
                            continue
                        v, sign = row[i]
                        if i == 0 and v is None:
                            dve.memset(now[:, n, :], float(sign))
                        elif i == 0:
                            dve.tensor_scalar(now[:, n, :], v, float(sign), None, ALU.mult)
                        else:
                            dve.tensor_tensor(now[:, n, :], now[:, n, :], v, ALU.add if sign > 0 else ALU.subtract)
            last = node[(NQ - 1) % 2]
            dve.drain()
            for q in range(NQ):
                (zn, zs), (xn, xs) = roots[q], roots[NQ + q]
                dve.scalar_tensor_tensor(out=term[:, 2 * q, :], in0=last[:, zn, :], scalar=float(zs),
                                         in1=c[:, 4, q, :], op0=ALU.mult, op1=ALU.mult)
                dve.scalar_tensor_tensor(out=term[:, 2 * q + 1, :], in0=last[:, xn, :], scalar=float(-xs),
                                         in1=s[:, 4, q, :], op0=ALU.mult, op1=ALU.mult)
            dve.drain()
            for q in range(NQ):
                dve.tensor_tensor(means[:, :, q], term[:, 2 * q, :], term[:, 2 * q + 1, :], ALU.add)
            dve.drain()

            def spread(b, u):
                wait(dve, turned, b - 1)
                dve.tensor_copy(mean4[u][:, :, :], means[:, bass.ds(b * 4, 4), :]).then_inc(mean_ready, 1)

            def embedded(b, u):
                dve.wait_ge(emb_mm, b + 1)
                wait(dve, emb_out[u], 8 * (b - u))
                dve.tensor_copy(emb[u][:, :, :].rearrange("p (a j) c -> p a (j c)", a=2),
                                e_ps[u][:, :, 0:2 * D]).then_inc(emb_ready, 1)

            pipeline(dve, B, 2, [(0, spread), (1, embedded)], peel=2)

NPAIR = B // 2


def product(pe, out, wa, wr, xs, m0, m1, tile):
    for h in range(2):
        t = slice(h * HL, (h + 1) * HL)
        for s in ((tile,) if tile < 2 else (0, 1)):
            r = slice(64 * s, 64 * s + 64)
            o = out[0:m1 - m0, h, 0:HL] if tile < 2 else out[r, h, 0:HL]
            pe.matmul(o, wa[:, m0:m1], xs[s][:, t], start=True, stop=False)
            mm = pe.matmul(o, wr[r, m0:m1], xs[2][r, t], start=False, stop=True,
                           tile_position=(64 * s, 64 * s if tile == 2 else 0))
    return mm


def ssm_inputs(nc, d, keep):
    with ExitStack() as ctx:
        def sb(name, shape, dt=F32):
            return ctx.enter_context(nc.sbuf_tensor("si_" + name, shape, dt))

        count = ctx.enter_context(semaphores(nc))

        def sem(name):
            return count("si_" + name)

        def kept_sem(name):
            return keep.enter_context(nc.semaphore("si_" + name))

        w_in_a, w_in_r = sb("w_in_a", [128, 2 * D]), sb("w_in_r", [128, 2 * D])
        w_dt_a, w_dt_r = sb("w_dt_a", [128, D]), sb("w_dt_r", [128, D])
        w_bc_a, w_bc_r = sb("w_bc_a", [128, 96]), sb("w_bc_r", [128, 96])
        chan = sb("chan", [128, 3, 6])
        part = sb("part", [96, 2])
        ident = sb("ident", [128, 128])
        h = [sb(f"h{i}", [TC, 2, NC, D]) for i in range(2)]
        stat = sb("stat", [TC, 2, NC, 6])
        mv = sb("mv", [TC, 2, NC, 2])
        root = sb("root", [TC, 2, NC])
        rstd = sb("rstd", [TC, 2, NC])
        na = sb("na", [TC, 2, NC, DA])
        nr = sb("nr", [TC, NC, 2, DR])
        xT = [[sb(f"xT{i}{k}", [128, L]) for k in range(3)] for i in range(2)]
        xpad = [[sb(f"xpad{i}{k}", [128, 3 + L]) for k in range(3)] for i in range(2)]
        conv = [[sb(f"conv{i}{k}", [128, L]) for k in range(3)] for i in range(2)]
        xs = [[sb(f"xs{i}{k}", [128, L]) for k in range(3)] for i in range(2)]
        sz = [[sb(f"sz{i}{k}", [128, L]) for k in range(3)] for i in range(2)]
        mag = [sb(f"mag{k}", [128, L]) for k in range(3)]
        dtt = [[sb(f"dt{i}{k}", [128, L]) for k in range(3)] for i in range(2)]
        p1 = sb("p1", [96, L], BF16)
        r1 = sb("r1", [96, L])
        p2 = sb("p2", [96, L], BF16)
        bc = [[sb(f"bc{i}{s}", [96, L], BF16) for s in range(2)] for i in range(2)]
        tr_ps = ctx.enter_context(nc.psum_tensor("si_tr_ps", [128, 2, 512], F32))
        xz_ps = [ctx.enter_context(nc.psum_tensor(f"si_xz_ps{i}", [128, 2, 512], F32)) for i in range(2)]
        db_ps = ctx.enter_context(nc.psum_tensor("si_db_ps", [128, 2, 512], F32))

        loaded, h_in, h_read = sem("loaded"), [kept_sem("h_in0"), kept_sem("h_in1")], sem("h_read")
        var_ready, root_ready, norm_ready = sem("var_ready"), sem("root_ready"), sem("norm_ready")
        tr_mm, tr_ready = sem("tr_mm"), sem("tr_ready")
        xz_mm, x_copied = sem("xz_mm"), sem("x_copied")
        conv_ready, xs_ready, z_ready = sem("conv_ready"), sem("xs_ready"), sem("z_ready")
        db_mm, v_ready, ln_ready = sem("db_mm"), sem("v_ready"), sem("ln_ready")
        dt_ready, bc_ready, bc_mm = sem("dt_ready"), sem("bc_ready"), sem("bc_mm")
        out1 = [sem("out1_0"), sem("out1_1")]
        out2 = [sem("out2_0"), sem("out2_1")]
        passed, pool_passed = sem("passed"), sem("pool_passed")
        N1, N2 = 16 * 6, 16 * 5
        groups = [(0, (0, 1, 2)), (0, (3, 4, 5)), (1, (0, 1, 2)), (1, (3, 4, 5)), (2, (0, 1, 2)), (2, (3, 4, 5))]
        NG = len(groups)
        block = ctx.enter_context(nc.Block())

        @block.sync
        def _(sp):
            for t, s in ((w_in_a, "w_in_a"), (w_in_r, "w_in_r"), (w_dt_a, "w_dt_a"), (w_dt_r, "w_dt_r"),
                         (w_bc_a, "w_bc_a"), (w_bc_r, "w_bc_r"), (part, "part"), (ident, "ident")):
                sp.dma_start(t[:, :], d[s]).then_inc(loaded, 16)
            sp.dma_start(chan[:, :, :], d["chan"]).then_inc(loaded, 16)

            def store1(p, u):
                for k in range(3):
                    wait_alone(sp, z_ready, 3 * p + k + 1, passed)
                    sp.dma_start(d["ssm_z"][bass.ds(p * 3 + k, 1), :, :].rearrange("o p t -> (o p) t"),
                                 sz[u][k][:, :]).then_inc(out1[u], 16)
                for k in range(3):
                    wait_alone(sp, xs_ready, 3 * p + k + 1, passed)
                    sp.dma_start(d["ssm_x"][bass.ds(p * 3 + k, 1), :, :].rearrange("o p t -> (o p) t"),
                                 xs[u][k][:, :]).then_inc(out1[u], 16)

            def store2(p, u):
                for k in range(3):
                    wait_alone(sp, dt_ready, 3 * p + k + 1, passed)
                    sp.dma_start(d["ssm_dt"][bass.ds(p * 3 + k, 1), :, :].rearrange("o p t -> (o p) t"),
                                 dtt[u][k][:, :]).then_inc(out2[u], 16)
                for s in range(2):
                    wait_alone(sp, bc_ready, 2 * p + s + 1, passed)
                    sp.dma_start(d["ssm_bc"][bass.ds(p * 2 + s, 1), :, :].rearrange("o p t -> (o p) t"),
                                 bc[u][s][:, :]).then_inc(out2[u], 16)

            pipeline(sp, NPAIR, 2, [(1, store1), (2, store2)], peel=2)
            for u in range(2):
                sp.wait_ge(out1[u], N1 * NPAIR // 2)
                sp.wait_ge(out2[u], N2 * NPAIR // 2)

        @block.gpsimd
        def _(pool):
            def load(p, u):
                wait_alone(pool, h_read, p - 1, pool_passed)
                pool.dma_start(h[u][:, :, :, :].rearrange("p s c w -> p (s c) w"),
                               d["h0"][bass.ds(p * 2, 2), :, :].rearrange("s (c p) w -> p (s c) w", p=TC)
                               ).then_inc(h_in[u], 16)

            pipeline(pool, NPAIR, 2, [(0, load)])

        @block.scalar
        def _(act):
            act.wait_ge(loaded, 16 * 9)

            def roots(p, u):
                act.wait_ge(var_ready, p + 1)
                act.activation(root[:, :, :], mv[:, :, :, 1], ACT.Sqrt).then_inc(root_ready, 1)

            def turned(p, u):
                wait(act, xz_mm, 6 * (p - 1))
                for n, (k, chunks) in enumerate(groups):
                    act.wait_ge(tr_mm, NG * p + n + 1)
                    act.activation(xT[u][k][:, chunks[0] * TC:(chunks[-1] + 1) * TC],
                                   tr_ps[:, n % 2, 0:3 * TC], ACT.Copy).then_inc(tr_ready, 1)

            def inputs(p, u):
                wait(act, conv_ready, 3 * (p - 1))
                for k in range(3):
                    act.wait_ge(xz_mm, 6 * p + k + 1)
                    act.activation(xpad[u][k][:, 3:3 + L].rearrange("p (h t) -> p h t", h=2),
                                   xz_ps[k % 2][:, :, 0:HL], ACT.Copy).then_inc(x_copied, 1)

            def gates(p, u):
                wait(act, out1[u], N1 * (p - u) // 2 if isinstance(p, int) else (p - u) * (N1 // 2))
                for k in range(3):
                    act.wait_ge(xz_mm, 6 * p + 3 + k + 1)
                    act.activation(sz[u][k][:, :].rearrange("p (h t) -> p h t", h=2),
                                   xz_ps[(3 + k) % 2][:, :, 0:HL], ACT.Silu).then_inc(z_ready, 1)
                wait(act, bc_mm, 2 * (p - 1))
                for k in range(3):
                    act.wait_ge(conv_ready, 3 * p + k + 1)
                    act.activation(xs[u][k][:, :], conv[u][k][:, :], ACT.Silu).then_inc(xs_ready, 1)

            def softplus(p, u):
                wait(act, dt_ready, 3 * p)
                for k in range(3):
                    act.wait_ge(v_ready, 3 * p + k + 1)
                    act.activation(mag[k][:, :], dtt[u][k][:, :], ACT.Abs)
                act.drain()
                for k in range(3):
                    act.activation(mag[k][:, :], mag[k][:, :], ACT.Exp, scale=-1.0)
                act.drain()
                for k in range(3):
                    act.activation(mag[k][:, :], mag[k][:, :], ACT.Ln, bias=1.0).then_inc(ln_ready, 1)

            pipeline(act, NPAIR, 2, [(1, turned), (0, roots), (1, inputs), (2, softplus), (1, gates)], peel=2)

        @block.tensor
        def _(pe):
            pe.wait_ge(loaded, 16 * 9)

            def turn(p, u):
                pe.wait_ge(norm_ready, p + 1)
                for n, (k, chunks) in enumerate(groups):
                    wait(pe, tr_ready, NG * p + n - 1)
                    for i, c in enumerate(chunks):
                        src = na[:, k, c, :] if k < 2 else nr[:, c, :, :].rearrange("p s w -> p (s w)")
                        mm = pe.transpose(tr_ps[:, n % 2, i * TC:(i + 1) * TC], src, ident[0:TC, 0:TC])
                    mm.then_inc(tr_mm, 1)
                pe.wait_ge(tr_ready, NG * (p + 1))

            def xz(p, u, n):
                if n in (0, 1):
                    wait(pe, z_ready, 3 * (p - 1) + n + 2)
                elif n in (2, 3, 4):
                    pe.wait_ge(x_copied, 3 * p + n - 1)
                else:
                    pe.wait_ge(z_ready, 3 * p + n - 4)
                m = D * (n // 3) + (0 if n % 3 < 2 else DA)
                product(pe, xz_ps[n % 2], w_in_a, w_in_r, xT[u], m, m + (DA if n % 3 < 2 else DR),
                        n % 3).then_inc(xz_mm, 1)

            def db_free(p, n):
                if n == 0:
                    wait(pe, bc_ready, 2 * p)
                elif n < 4:
                    pe.wait_ge(v_ready, 3 * p + n)
                else:
                    pe.wait_ge(bc_ready, 2 * p + 1)

            def dt(p, u, k):
                pe.wait_ge(xs_ready, 3 * p + 3)
                db_free(p, k)
                m = 0 if k < 2 else DA
                product(pe, db_ps, w_dt_a, w_dt_r, xs[u], m, m + (DA if k < 2 else DR), k).then_inc(db_mm, 1)

            def bc_(p, u, s):
                db_free(p, 3 + s)
                product(pe, db_ps, w_bc_a, w_bc_r, xs[u], 0, 96, s)
                pe.drain().then_inc(db_mm, 1)
                pe.sem_inc(bc_mm, 1)

            def back(n):
                return lambda p, u: dt(p, u, n) if n < 3 else bc_(p, u, n - 3)

            def front(n):
                return lambda p, u: xz(p, u, n)

            pipeline(pe, NPAIR, 2, [(1, turn), (1, front(0)), (1, front(1)), (2, back(0)), (2, back(1)), (1, front(2)),
                                    (2, back(2)), (1, front(3)), (2, back(3)), (1, front(4)), (2, back(4)),
                                    (1, front(5))], peel=2)

        @block.vector
        def _(dve):
            for i in range(2):
                for k in range(3):
                    dve.memset(xpad[i][k][:, 0:3], 0.0)
            dve.wait_ge(loaded, 16 * 9)

            def norm(p, u):
                dve.wait_ge(h_in[u], (p - u) * 8 + 16)
                for s in range(2):
                    for c in range(NC):
                        dve.bn_stats(stat[:, s, c, :], h[u][:, s, c, :])
                dve.drain()
                for s in range(2):
                    for c in range(NC):
                        dve.bn_aggr(mv[:, s, c, :], stat[:, s, c, :])
                dve.drain()
                dve.tensor_scalar(mv[:, :, :, 1], mv[:, :, :, 1], EPS, None, ALU.add).then_inc(var_ready, 1)
                dve.wait_ge(root_ready, p + 1)
                wait(dve, tr_mm, NG * p)
                dve.reciprocal(rstd[:, :, :], root[:, :, :])
                dve.drain()
                for s in range(2):
                    for c in range(NC):
                        m, r = mv[:, s, c, 0:1], rstd[:, s, c:c + 1]
                        dve.tensor_scalar(na[:, s, c, :], h[u][:, s, c, 0:DA], m, r, ALU.subtract, ALU.mult)
                        dve.tensor_scalar(nr[:, c, s, :], h[u][:, s, c, DA:D], m, r, ALU.subtract, ALU.mult)
                dve.drain().then_inc(norm_ready, 1)
                dve.sem_inc(h_read, 1)

            def convolve(k):
                def f(p, u):
                    wait(dve, xs_ready, 3 * (p - 1))
                    dve.wait_ge(x_copied, 3 * p + k + 1)
                    x, o = xpad[u][k], conv[u][k]
                    dve.tensor_scalar(o[:, :], x[:, 0:L], chan[:, k, 0:1], chan[:, k, 4:5], ALU.mult, ALU.add)
                    for tap in range(1, 4):
                        dve.drain()
                        i = dve.scalar_tensor_tensor(out=o[:, :], in0=x[:, tap:tap + L],
                                                     scalar=chan[:, k, tap:tap + 1],
                                                     in1=o[:, :], op0=ALU.mult, op1=ALU.add)
                    i.then_inc(conv_ready, 1)
                return f

            def before_softplus(k):
                def f(p, u):
                    wait(dve, out2[u], (p - u) * (N2 // 2))
                    dve.wait_ge(db_mm, 5 * p + k + 1)
                    dve.tensor_scalar(dtt[u][k][:, :].rearrange("p (h t) -> p h t", h=2), db_ps[:, :, 0:HL],
                                      chan[:, k, 5:6], None, ALU.add).then_inc(v_ready, 1)
                return f

            def split(p, u):
                for s in range(2):
                    dve.wait_ge(db_mm, 5 * p + 3 + s + 1)
                    x = db_ps[0:96, :, 0:HL]
                    v = lambda t: t[:, :].rearrange("p (h t) -> p h t", h=2)
                    dve.tensor_copy(v(p1), x)
                    dve.drain()
                    dve.scalar_tensor_tensor(out=v(r1), in0=v(p1), scalar=part[:, 0:1], in1=x,
                                             op0=ALU.mult, op1=ALU.add)
                    dve.drain()
                    dve.tensor_copy(p2[:, :], r1[:, :])
                    dve.drain()
                    dve.scalar_tensor_tensor(out=bc[u][s][:, :], in0=p2[:, :], scalar=part[:, 1:2], in1=r1[:, :],
                                             op0=ALU.mult, op1=ALU.add).then_inc(bc_ready, 1)

            def sum_dt(p, u):
                for k in range(3):
                    dve.wait_ge(ln_ready, 3 * p + k + 1)
                    dve.scalar_tensor_tensor(out=dtt[u][k][:, :], in0=dtt[u][k][:, :], scalar=0.0, in1=mag[k][:, :],
                                             op0=ALU.max, op1=ALU.add).then_inc(dt_ready, 1)

            pipeline(dve, NPAIR, 2, [(0, norm), (1, convolve(0)), (2, before_softplus(0)), (1, convolve(1)),
                                     (2, before_softplus(1)), (1, convolve(2)), (2, before_softplus(2)),
                                     (2, split), (2, sum_dt)], peel=2)

STEPS = 3 * NS


def over_steps(eng, parts):
    def pair_steps(p, first):
        for j in range(STEPS):
            for lag, f in parts:
                if j >= lag:
                    f(p, j - lag)
                elif not first:
                    f(p - 1, j - lag + STEPS)

    pair_steps(0, True)
    pair_steps(1, False)
    with eng.Fori(2, NPAIR) as p:
        pair_steps(p, False)
    for j in range(max(lag for lag, _ in parts)):
        for lag, f in parts:
            if j < lag:
                f(NPAIR - 1, j - lag + STEPS)


def ssm_scan(nc, d):
    with ExitStack() as ctx:
        def sb(name, shape, dt=F32):
            return ctx.enter_context(nc.sbuf_tensor("sc_" + name, shape, dt))

        count = ctx.enter_context(semaphores(nc))

        def sem(name):
            return count("sc_" + name)

        a_neg = sb("a_neg", [128, 3, NS])
        skip = sb("skip", [128, 3])
        ident = sb("ident", [128, 128])
        own_row = sb("own_row", [96, 2 * NS])
        select = sb("select", [96, 2 * NS, 128], BF16)
        x = [sb(f"x{k}", [128, L]) for k in range(3)]
        z = [sb(f"z{k}", [128, L]) for k in range(3)]
        dt = [sb(f"dt{k}", [128, L]) for k in range(3)]
        b_rows = [sb(f"b_rows{s}", [96, L], BF16) for s in range(2)]
        c_rows = [sb(f"c_rows{s}", [96, L], BF16) for s in range(2)]
        decay = [sb(f"decay{i}", [128, L]) for i in range(2)]
        b_all = [sb(f"b_all{i}", [128, L]) for i in range(2)]
        drive = [sb(f"drive{i}", [128, L]) for i in range(2)]
        state = [sb(f"state{i}", [128, L]) for i in range(2)]
        out = [sb(f"out{i}", [128, L]) for i in range(4)]
        y = [sb(f"y{k}", [128, L]) for k in range(3)]
        b_ps = ctx.enter_context(nc.psum_tensor("sc_b_ps", [128, 2, 512], F32))
        c_ps = [ctx.enter_context(nc.psum_tensor(f"sc_c_ps{i}", [128, 2, 512], F32)) for i in range(2)]
        y_ps = ctx.enter_context(nc.psum_tensor("sc_y_ps", [128, 2, 512], F32))

        loaded, a_ready, select_ready = sem("loaded"), sem("a_ready"), sem("select_ready")
        tile_in = [sem(f"tile_in{k}") for k in range(3)]
        b_in, c_in = sem("b_in"), sem("c_in")
        b_mm, c_mm, y_mm = sem("b_mm"), sem("c_mm"), sem("y_mm")
        b_copied, decay_ready = sem("b_copied"), sem("decay_ready")
        drive_ready, state_ready = sem("drive_ready"), sem("state_ready")
        out_ready = sem("out_ready")
        y_read, y_ready, y_out = sem("y_read"), sem("y_ready"), [sem(f"y_out{k}") for k in range(3)]
        passed, pool_passed = sem("passed"), sem("pool_passed")

        def count(p, j):
            return p * STEPS + j + 1

        def halves(t):
            return t[:, :].rearrange("p (h t) -> p h t", h=2)

        block = ctx.enter_context(nc.Block())

        @block.sync
        def _(sp):
            sp.dma_start(a_neg[:, :, :], d["a_log"]).then_inc(loaded, 16)
            sp.dma_start(own_row[:, :], d["own_row"]).then_inc(loaded, 16)
            sp.dma_start(skip[:, :], d["skip"]).then_inc(loaded, 16)
            sp.dma_start(ident[:, :], d["ident"]).then_inc(loaded, 16)

            def load_bc(p):
                for rows, used, landed in ((b_rows, b_mm, b_in), (c_rows, c_mm, c_in)):
                    wait_alone(sp, used, p * STEPS, passed)
                    for s in range(2):
                        sp.dma_start(rows[s][:, :], d["ssm_bc"][bass.ds(p * 2 + s, 1), :, :].rearrange(
                            "o p t -> (o p) t")).then_inc(landed, 16)

            def load(p, k):
                wait_alone(sp, y_ready, (p - 1) * 3 + k + 1, passed)
                for t, name in ((x[k], "ssm_x"), (dt[k], "ssm_dt"), (z[k], "ssm_z")):
                    sp.dma_start(t[:, :], d[name][bass.ds(p * 3 + k, 1), :, :].rearrange("o p t -> (o p) t")
                                 ).then_inc(tile_in[k], 16)

            def store(p, k):
                wait_alone(sp, y_ready, p * 3 + k + 1, passed)
                sp.dma_start(d["ssm_y"][bass.ds(p * 3 + k, 1), :, :].rearrange("o p t -> (o p) t"),
                             y[k][:, :]).then_inc(y_out[k], 16)

            load_bc(0)
            for k in range(3):
                load(0, k)
            with sp.Fori(1, NPAIR) as p:
                for k in range(3):
                    load(p, k)
                    store(p - 1, k)
                    if k == 1:
                        load_bc(p)
            for k in range(3):
                store(NPAIR - 1, k)
            for k in range(3):
                sp.wait_ge(y_out[k], 16 * NPAIR)

        @block.scalar
        def _(act):
            act.wait_ge(loaded, 64)
            act.activation(a_neg[:, :, :], a_neg[:, :, :], ACT.Exp).then_inc(a_ready, 1)
            act.wait_ge(a_ready, 2)

            def spread_b(p, j):
                act.wait_ge(b_mm, count(p, j))
                wait(act, drive_ready, count(p, j) - 2)
                act.activation(halves(b_all[j % 2]), b_ps[:, :, 0:HL], ACT.Copy).then_inc(b_copied, 1)

            def decays(p, j):
                k, n = divmod(j, NS)
                if n == 0:
                    act.wait_ge(tile_in[k], (p + 1) * 48)
                wait(act, state_ready, count(p, j) - 2)
                act.activation(decay[j % 2][:, :], dt[k][:, :], ACT.Exp,
                               scale=a_neg[:, k, n:n + 1]).then_inc(decay_ready, 1)

            over_steps(act, [(0, spread_b), (0, decays)])

        @block.gpsimd
        def _(pool):
            def drives(p, j):
                k, n = divmod(j, NS)
                if n == 0:
                    wait_alone(pool, tile_in[k], (p + 1) * 48, pool_passed)
                wait_alone(pool, b_copied, count(p, j), pool_passed)
                wait_alone(pool, state_ready, count(p, j) - 2, pool_passed)
                pool.tensor_tensor(drive[j % 2][:, :], x[k][:, :], b_all[j % 2][:, :], ALU.mult).then_inc(drive_ready, 1)

            over_steps(pool, [(0, drives)])

        @block.tensor
        def _(pe):
            pe.wait_ge(loaded, 64)
            pe.wait_ge(select_ready, 1)

            def spread(ps_, bc, j, row):
                k = j // NS
                for h in range(2):
                    t = slice(h * HL, (h + 1) * HL)
                    if k < 2:
                        mm = pe.matmul(ps_[:, h, 0:HL], select[:, row, :], bc[k][:, t], start=True, stop=True)
                    else:
                        for s in range(2):
                            r = slice(64 * s, 64 * s + 64)
                            mm = pe.matmul(ps_[r, h, 0:HL], select[:, row, 0:64], bc[s][:, t], start=True, stop=True)
                return mm

            def spread_b(p, j):
                wait(pe, b_copied, count(p, j) - 1)
                if j == 0:
                    pe.wait_ge(b_in, (p + 1) * 32)
                spread(b_ps, b_rows, j, j % NS).then_inc(b_mm, 1)

            def spread_c(p, j):
                wait(pe, out_ready, count(p, j) - 2)
                if j == 0:
                    pe.wait_ge(c_in, (p + 1) * 32)
                spread(c_ps[j % 2], c_rows, j, NS + j % NS).then_inc(c_mm, 1)

            def sums(p, j):
                k, n = divmod(j, NS)
                pe.wait_ge(out_ready, count(p, j))
                if n == 0:
                    wait(pe, y_read, p * 3 + k)
                for h in range(2):
                    mm = pe.matmul(y_ps[:, h, 0:HL], ident[:, :], out[j % 4][:, h * HL:(h + 1) * HL],
                                   start=(n == 0), stop=(n == NS - 1))
                mm.then_inc(y_mm, 1)

            over_steps(pe, [(1, spread_c), (0, spread_b), (4, sums)])

        @block.vector
        def _(dve):
            dve.wait_ge(loaded, 64)
            dve.tensor_copy(select[:, :, :], own_row[:, :].unsqueeze(2).to_broadcast([96, 2 * NS, 128])
                            ).then_inc(select_ready, 1)
            dve.wait_ge(a_ready, 1)
            dve.tensor_scalar(a_neg[:, :, :], a_neg[:, :, :], -1.0, None, ALU.mult).then_inc(a_ready, 1)

            def scan(p, j):
                dve.wait_ge(decay_ready, count(p, j))
                dve.wait_ge(drive_ready, count(p, j))
                wait(dve, out_ready, count(p, j) - 2)
                dve.tensor_tensor_scan(state[j % 2][:, :], decay[j % 2][:, :], drive[j % 2][:, :], 0.0,
                                       ALU.mult, ALU.add).then_inc(state_ready, 1)

            def times_c(p, j):
                dve.wait_ge(c_mm, count(p, j))
                wait(dve, y_mm, count(p, j) - 4)
                dve.wait_ge(state_ready, count(p, j))
                dve.tensor_tensor(halves(out[j % 4]), halves(state[j % 2]), c_ps[j % 2][:, :, 0:HL],
                                  ALU.mult).then_inc(out_ready, 1)

            def finish(p, j):
                k, n = divmod(j, NS)
                if n == NS - 1:
                    dve.wait_ge(y_mm, count(p, j))
                    wait(dve, y_out[k], p * 16)
                    dve.scalar_tensor_tensor(out=halves(y[k]), in0=halves(x[k]), scalar=skip[:, k:k + 1],
                                             in1=y_ps[:, :, 0:HL], op0=ALU.mult, op1=ALU.add).then_inc(y_read, 1)
                    dve.drain()
                    dve.tensor_tensor(y[k][:, :], y[k][:, :], z[k][:, :], ALU.mult).then_inc(y_ready, 1)

            over_steps(dve, [(4, finish), (0, scan), (0, times_c)])


def route(nc, d, keep):
    TURN = 4
    with ExitStack() as ctx:
        def sb(name, shape, dt=F32):
            return ctx.enter_context(nc.sbuf_tensor("rt_" + name, shape, dt))

        count = ctx.enter_context(semaphores(nc))

        def sem(name):
            return count("rt_" + name)

        def kept_sem(name):
            return keep.enter_context(nc.semaphore("rt_" + name))

        def ps(name, shape):
            return ctx.enter_context(nc.psum_tensor("rt_" + name, shape, F32))

        K = 2 * NC
        w_a, w_r = sb("w_a", [128, D]), sb("w_r", [128, D])
        router_a, router_r = sb("router_a", [128, E]), sb("router_r", [DR, E])
        ident = sb("ident", [128, 128])
        upper32 = sb("upper32", [TC, TC])
        upper = sb("upper", [TC, TC], BF16)
        ones = sb("ones", [TC, TC], BF16)
        rank = sb("rank", [TC, NC, E])
        first_slot = sb("first_slot", [TC, K, E])
        trash = sb("trash", [TC, K])
        base = sb("base", [TC, 1])
        h0 = [sb(f"h0{i}", [TC, NC, D]) for i in range(TURN)]
        y_a = [sb(f"y_a{i}", [128, L]) for i in range(TURN)]
        y_r = [sb(f"y_r{i}", [128, L]) for i in range(TURN)]
        stat, mv = sb("stat", [TC, NC, 6]), sb("mv", [TC, NC, 2])
        root, rstd = sb("root", [TC, NC]), sb("rstd", [TC, NC])
        xn = [sb(f"xn{i}", [TC, NC, D]) for i in range(TURN)]
        xT_a, xT_r = [sb(f"xT_a{i}", [128, L]) for i in range(2)], [sb(f"xT_r{i}", [DR, L]) for i in range(2)]
        logit = [sb(f"logit{i}", [TC, NC, E]) for i in range(2)]
        expo = [sb(f"expo{i}", [TC, NC, E]) for i in range(2)]
        m = sb("m", [TC, NC])
        total = sb("total", [TC, NC])
        prob, rest = sb("prob", [TC, NC, E]), sb("rest", [TC, NC, E])
        eq = sb("eq", [TC, NC, E])
        gate = [sb(f"gate{i}", [TC, K]) for i in range(2)]
        hot = [sb(f"hot{i}", [TC, K, E]) for i in range(2)]
        hot16 = [sb(f"hot16{i}", [TC, K, E], BF16) for i in range(2)]
        pick, pick2 = sb("pick", [TC, K, E]), sb("pick2", [TC, K, E])
        pos, slot, valid = sb("pos", [TC, K]), sb("slot", [TC, K]), sb("valid", [TC, K])
        scat_f, gath_f = sb("scat_f", [TC, K]), sb("gath_f", [TC, K])
        scat = [sb(f"scat{i}", [TC, K], I32) for i in range(2)]
        gath = [sb(f"gath{i}", [TC, K], I32) for i in range(2)]
        weight = [sb(f"weight{i}", [TC, K]) for i in range(2)]
        o_ps = [ps(f"o_ps{i}", [TC, 512]) for i in range(2)]
        t_ps = [ps(f"t_ps{i}", [128, 512]) for i in range(2)]
        l_ps = ps("l_ps", [TC, NC, E])
        c_ps = ps("c_ps", [TC, K, E])

        loaded = sem("loaded")
        ones_ready, upper_ready = sem("ones_ready"), sem("upper_ready")
        h_in = [sem(f"h_in{i}") for i in range(TURN)]
        h1_out = [sem(f"h1_out{i}") for i in range(TURN)]
        o_mm, o_read = sem("o_mm"), sem("o_read")
        h1_ready, var_ready, root_ready, norm_ready = sem("h1_ready"), sem("var_ready"), sem("root_ready"), sem("norm_ready")
        t_mm, t_ready = sem("t_mm"), sem("t_ready")
        l_mm, logit_ready, exp_ready = sem("l_mm"), sem("logit_ready"), sem("exp_ready")
        exp_read = sem("exp_read")
        hot_ready, c_mm, place_ready = sem("hot_ready"), sem("c_mm"), sem("place_ready")
        scattered = [kept_sem(f"scattered{i}") for i in range(2)]
        tables_out = [sem(f"tables_out{i}") for i in range(2)]
        passed, pool_passed, pe_passed = sem("passed"), sem("pool_passed"), sem("pe_passed")
        OG, TG = NC // 2, 4
        block = ctx.enter_context(nc.Block())

        @block.sync
        def _(sp):
            consts = ((w_a, "w_out_a"), (w_r, "w_out_r"), (router_a, "router_a"), (router_r, "router_r"),
                      (ident, "ident"), (upper32, "upper"), (trash, "trash"))
            for t, s in consts:
                sp.dma_start(t[:, :], d[s]).then_inc(loaded, 16)
            sp.dma_start(rank[:, :, :], d["rank"]).then_inc(loaded, 16)
            sp.dma_start(first_slot[:, :, :], d["first_slot"]).then_inc(loaded, 16)

            def load(b, u):
                wait_alone(sp, h1_ready, b - TURN + 1, passed)
                wait_alone(sp, o_mm, OG * (b - TURN + 1), passed)
                wait_alone(sp, h1_out[u], (b - u) * (16 // TURN), passed)
                sp.dma_start(h0[u][:, :, :], d["h0"][bass.ds(b, 1), :, :].rearrange(
                    "o (c p) w -> p (o c) w", p=TC)).then_inc(h_in[u], 16)
                s = u % 2
                at = (b - s) // 2 * 3 if isinstance(b, int) else (b - s) * 3 // 2
                sp.dma_start(y_a[u][:, :], d["ssm_y"][bass.ds(at + s, 1), :, :].rearrange(
                    "o p t -> (o p) t")).then_inc(h_in[u], 16)
                sp.dma_start(y_r[u][64 * s:64 * s + 64, :], d["ssm_y"][bass.ds(at + 2, 1), 64 * s:64 * s + 64, :].rearrange(
                    "o p t -> (o p) t")).then_inc(h_in[u], 16)

            def store_h1(b, u):
                wait_alone(sp, h1_ready, b + 1, passed)
                sp.dma_start(d["h1"][bass.ds(b, 1), :, :].rearrange("o (c p) w -> p (o c) w", p=TC),
                             h0[u][:, :, :]).then_inc(h1_out[u], 16)

            def store_tables(b, u):
                wait_alone(sp, place_ready, b + 1, passed)
                sp.dma_start(d["rt_index"][bass.ds(b, 1), :, :].rearrange("o p k -> (o p) k"),
                             gath[u % 2][:, :]).then_inc(tables_out[u % 2], 16)
                sp.dma_start(d["rt_weight"][bass.ds(b, 1), :, :].rearrange("o p k -> (o p) k"),
                             weight[u % 2][:, :]).then_inc(tables_out[u % 2], 16)

            pipeline(sp, B, TURN, [(0, load), (2, store_h1), (4, store_tables)], peel=2)
            for u in range(TURN):
                sp.wait_ge(h1_out[u], 16 * B // TURN)
            for u in range(2):
                sp.wait_ge(tables_out[u], 32 * B // 2)

        @block.gpsimd
        def _(pool):
            pool.memset(ones[:, :], 1.0)
            pool.drain().then_inc(ones_ready, 1)

            def scatter(b, u):
                wait_alone(pool, place_ready, b + 1, pool_passed)
                for k in range(K):
                    pool.indirect_dma_start(
                        out=d["xin"], out_offset=bass.IndirectOffsetOnAxis(ap=scat[u % 2][:, k:k + 1], axis=0),
                        in_=xn[u][:, k % NC, :], in_offset=None).then_inc(scattered[u % 2], 16)

            pipeline(pool, B, TURN, [(4, scatter)], peel=2)
            for u in range(2):
                pool.wait_ge(scattered[u], K * 16 * B // 2)

        @block.scalar
        def _(act):
            def roots(b, u):
                act.wait_ge(var_ready, b + 1)
                act.activation(root[:, :], mv[:, :, 1], ACT.Sqrt).then_inc(root_ready, 1)

            def turned(b, u):
                wait(act, l_mm, b - 1)
                for g in range(TG):
                    act.wait_ge(t_mm, TG * b + g + 1)
                    dst = xT_a[u % 2] if g < 2 else xT_r[u % 2]
                    act.activation(dst[:, g % 2 * 3 * TC:(g % 2 + 1) * 3 * TC],
                                   t_ps[g % 2][0:(DA if g < 2 else DR), 0:3 * TC], ACT.Copy).then_inc(t_ready, 1)

            def exponentials(b, u):
                act.wait_ge(logit_ready, b + 1)
                wait(act, exp_read, b - 1)
                act.activation(expo[u % 2][:, :, :], logit[u % 2][:, :, :], ACT.Exp).then_inc(exp_ready, 1)

            pipeline(act, B, TURN, [(1, roots), (2, turned), (3, exponentials)], peel=2)

        @block.tensor
        def _(pe):
            pe.wait_ge(loaded, 16 * 9)
            pe.wait_ge(ones_ready, 1)
            pe.wait_ge(upper_ready, 1)

            def project(b, u):
                pe.wait_ge(h_in[u], ((b - u) // TURN + 1) * 48 if isinstance(b, int) else (b - u + TURN) * (48 // TURN))
                s = slice(64 * (u % 2), 64 * (u % 2) + 64)
                for g in range(OG):
                    wait(pe, o_read, OG * b + g - 1)
                    for i in range(2):
                        c = 2 * g + i
                        o = o_ps[(OG * u + g) % 2][:, i * D:(i + 1) * D]
                        t = slice(c * TC, (c + 1) * TC)
                        pe.matmul(o, y_a[u][:, t], w_a[:, :], start=True, stop=False)
                        mm = pe.matmul(o, y_r[u][s, t], w_r[s, :], start=False, stop=True)
                    mm.then_inc(o_mm, 1)

            def turn_(b, u):
                pe.wait_ge(norm_ready, b + 1)
                for g in range(TG):
                    if g < 2:
                        wait(pe, t_ready, TG * b + g - 1)
                    else:
                        wait_alone(pe, t_ready, TG * b + g - 1, pe_passed)
                    for i in range(3):
                        c = g % 2 * 3 + i
                        src = xn[u][:, c, 0:DA] if g < 2 else xn[u][:, c, DA:D]
                        mm = pe.transpose(t_ps[g % 2][0:(DA if g < 2 else DR), i * TC:(i + 1) * TC], src,
                                          ident[0:TC, 0:TC])
                    mm.then_inc(t_mm, 1)

            def logits(b, u):
                pe.wait_ge(t_ready, TG * (b + 1))
                wait(pe, logit_ready, b)
                for c in range(NC):
                    t = slice(c * TC, (c + 1) * TC)
                    pe.matmul(l_ps[:, c, :], xT_a[u % 2][:, t], router_a[:, :], start=True, stop=False)
                    mm = pe.matmul(l_ps[:, c, :], xT_r[u % 2][:, t], router_r[:, :], start=False, stop=True)
                mm.then_inc(l_mm, 1)

            def counts(b, u):
                pe.wait_ge(hot_ready, b + 1)
                wait(pe, place_ready, b)
                h = hot16[u % 2]
                mm = pe.matmul(c_ps[:, :, :], upper[:, :], h[:, :, :], start=True, stop=False)
                for s in range(1, K):
                    mm = pe.matmul(c_ps[:, s:K, :], ones[:, :], h[:, 0:K - s, :], start=False, stop=(s == K - 1))
                mm.then_inc(c_mm, 1)

            pipeline(pe, B, TURN, [(1, project), (4, counts), (3, logits), (2, turn_)], peel=2)

        @block.vector
        def _(dve):
            dve.memset(base[:, :], 0.0)
            dve.wait_ge(loaded, 16 * 9)
            dve.tensor_copy(upper[:, :], upper32[:, :]).then_inc(upper_ready, 1)

            def normalize(b, u):
                h = h0[u]
                for g in range(OG):
                    dve.wait_ge(o_mm, OG * b + g + 1)
                    x = h[:, 2 * g:2 * g + 2, :].rearrange("p c w -> p (c w)")
                    dve.tensor_tensor(x, x, o_ps[(OG * u + g) % 2][:, 0:2 * D], ALU.add).then_inc(o_read, 1)
                dve.drain()
                statistics(dve, h, stat, mv).then_inc(var_ready, 1)
                dve.wait_ge(root_ready, b + 1)
                dve.reciprocal(rstd[:, :], root[:, :])
                dve.drain()
                v = scattered[u % 2]
                if isinstance(b, int):
                    wait(dve, v, ((b - TURN) // 2 + 1) * K * 16)
                else:
                    dve.wait_ge(v, (b - u % 2 - TURN + 2) * (K * 16 // 2))
                for c in range(NC):
                    dve.tensor_scalar(xn[u][:, c, :], h[:, c, :], mv[:, c, 0:1], rstd[:, c:c + 1], ALU.subtract, ALU.mult)
                dve.drain().then_inc(norm_ready, 1)
                dve.sem_inc(h1_ready, 1)

            def over_experts(t, n=NC):
                return t.unsqueeze(2).to_broadcast([TC, n, E])

            def shifted(b, u):
                dve.wait_ge(l_mm, b + 1)
                wait(dve, exp_ready, b - 1)
                dve.tensor_reduce(m[:, :], l_ps[:, :, :], AX.X, ALU.max)
                dve.drain()
                dve.tensor_tensor(logit[u % 2][:, :, :], l_ps[:, :, :], over_experts(m[:, :]),
                                  ALU.subtract).then_inc(logit_ready, 1)

            def choose(p, g, hot_, u):
                dve.tensor_reduce(g, p, AX.X, ALU.max)
                dve.drain()
                dve.tensor_tensor(eq[:, :, :], p, over_experts(g), ALU.is_equal)
                dve.drain()
                dve.tensor_tensor(eq[:, :, :], eq[:, :, :], rank[:, :, :], ALU.mult)
                dve.drain()
                dve.tensor_reduce(m[:, :], eq[:, :, :], AX.X, ALU.max)
                dve.drain()
                dve.tensor_tensor(hot_, eq[:, :, :], over_experts(m[:, :]), ALU.is_equal)
                dve.drain()

            def choices(b, u):
                v = u % 2
                dve.wait_ge(exp_ready, b + 1)
                dve.tensor_reduce(total[:, :], expo[v][:, :, :], AX.X, ALU.add)
                dve.drain()
                dve.reciprocal(total[:, :], total[:, :])
                dve.drain()
                dve.tensor_tensor(prob[:, :, :], expo[v][:, :, :], over_experts(total[:, :]), ALU.mult).then_inc(exp_read, 1)
                dve.drain()
                choose(prob[:, :, :], gate[v][:, 0:NC], hot[v][:, 0:NC, :], u)
                dve.scalar_tensor_tensor(out=rest[:, :, :], in0=hot[v][:, 0:NC, :], scalar=-2.0, in1=prob[:, :, :],
                                         op0=ALU.mult, op1=ALU.add)
                dve.drain()
                choose(rest[:, :, :], gate[v][:, NC:K], hot[v][:, NC:K, :], u)
                wait(dve, c_mm, b - 1)
                dve.tensor_copy(hot16[v][:, :, :], hot[v][:, :, :]).then_inc(hot_ready, 1)

            def places(b, u):
                v = u % 2
                dve.wait_ge(c_mm, b + 1)
                if isinstance(b, int):
                    wait(dve, scattered[v], b // 2 * K * 16)
                    wait(dve, tables_out[v], b // 2 * 32)
                else:
                    dve.wait_ge(scattered[v], (b - v) * (K * 16 // 2))
                    dve.wait_ge(tables_out[v], (b - v) * 16)
                dve.tensor_tensor(pick[:, :, :], hot[v][:, :, :], c_ps[:, :, :], ALU.mult)
                dve.tensor_tensor(pick2[:, :, :], hot[v][:, :, :], first_slot[:, :, :], ALU.mult)
                dve.drain()
                dve.tensor_reduce(pos[:, :], pick[:, :, :], AX.X, ALU.add)
                dve.tensor_reduce(slot[:, :], pick2[:, :, :], AX.X, ALU.add)
                dve.drain()
                dve.tensor_scalar(valid[:, :], pos[:, :], float(CAP), None, ALU.is_le)
                dve.scalar_tensor_tensor(out=slot[:, :], in0=pos[:, :], scalar=-1.0, in1=slot[:, :],
                                         op0=ALU.add, op1=ALU.add)
                dve.drain()
                dve.tensor_tensor(gath_f[:, :], slot[:, :], valid[:, :], ALU.mult)
                dve.tensor_tensor(weight[v][:, :], gate[v][:, :], valid[:, :], ALU.mult)
                dve.scalar_tensor_tensor(out=scat_f[:, :], in0=slot[:, :], scalar=base[:, :], in1=trash[:, :],
                                         op0=ALU.add, op1=ALU.subtract)
                dve.drain()
                dve.tensor_tensor(scat_f[:, :], scat_f[:, :], valid[:, :], ALU.mult)
                dve.tensor_scalar(gath[v][:, :], gath_f[:, :], base[:, :], None, ALU.add)
                dve.drain()
                dve.tensor_tensor(scat[v][:, :], scat_f[:, :], trash[:, :], ALU.add)
                dve.drain()
                dve.tensor_scalar(base[:, :], base[:, :], float(SLOT), None, ALU.add)
                dve.tensor_scalar(trash[:, :], trash[:, :], float(TRASH), None, ALU.add)
                dve.drain().then_inc(place_ready, 1)

            pipeline(dve, B, TURN, [(4, choices), (1, normalize), (4, places), (3, shifted)], peel=2)


def experts(nc, d):
    UP, XG = FC // 2, (XCH - 1) // 4
    NG = 2 * XG + 1
    OW = (CAP + 1) // 2
    with ExitStack() as ctx:
        def sb(name, shape, dt=F32):
            return ctx.enter_context(nc.sbuf_tensor("ex_" + name, shape, dt))

        count = ctx.enter_context(semaphores(nc))

        def sem(name):
            return count("ex_" + name)

        def ps(name, shape):
            return ctx.enter_context(nc.psum_tensor("ex_" + name, shape, F32))

        wi_a = sb("wi_a", [128, E, F])
        wi_r = sb("wi_r", [128, E, UP, 128])
        wo = sb("wo", [128, E, FC, D])
        ident = sb("ident", [128, 128])
        x = [sb(f"x{i}", [XROWS, XCH, 256]) for i in range(2)]
        xT = [sb(f"xT{i}", [128, 2, SLOT]) for i in range(2)]
        hT = [sb(f"hT{i}", [128, FC, CAP]) for i in range(2)]
        o = [sb(f"o{i}", [OW, E, 2, D]) for i in range(2)]
        t_ps = [ps(f"t_ps{i}", [128, 512]) for i in range(2)]
        h_ps = [ps(f"h_ps{i}", [128, 2, 512]) for i in range(2)]
        o_ps = [ps(f"o_ps{i}", [OW, 512]) for i in range(2)]

        w_in = [sem(f"w_in{e}") for e in range(E)]
        ident_in = sem("ident_in")
        x_in = [sem(f"x_in{i}") for i in range(2)]
        o_out = [sem(f"o_out{i}") for i in range(2)]
        t_mm, t_ready, u_mm, d_mm = sem("t_mm"), sem("t_ready"), sem("u_mm"), sem("d_mm")
        h_even, h_odd, o_ready = sem("h_even"), sem("h_odd"), sem("o_ready")
        passed = sem("passed")

        def groups(e):
            return [e] if e < E - 1 else [e, e + 1]

        def over_experts(eng, parts):
            turn = 2 * E

            def units(b0, first):
                for j in range(turn):
                    for lag, f in parts:
                        if j >= lag or not first:
                            f(b0 + (j - lag) // E, (j - lag) % E, (j - lag) // E % 2)

            units(0, True)
            units(2, False)
            with eng.Fori(2, B // 2) as i:
                units(i * 2, False)
            for j in range(max(lag for lag, _ in parts)):
                for lag, f in parts:
                    if j < lag:
                        f(B + (j - lag) // E, (j - lag) % E, (j - lag) // E % 2)

        assert NG == E + 1 and SLOT == XCH * XROWS and XCH == 4 * XG + 1
        block = ctx.enter_context(nc.Block())

        @block.sync
        def _(sp):
            sp.dma_start(ident[:, :], d["ident"]).then_inc(ident_in, 16)

            def load(b, u):
                wait_alone(sp, t_mm, NG * (b - 1), passed)
                rows = d["xin"][bass.ds(b * SLOT, SLOT), :].rearrange("(c p) w -> p c w", p=XROWS)
                sp.dma_start(x[u][:, :, 0:D], rows).then_inc(x_in[u], 16)
                sp.dma_start(x[u][:, :, D:256], rows[:, :, DA:D]).then_inc(x_in[u], 16)

            def store(b, u):
                wait_alone(sp, o_ready, E * (b + 1), passed)
                rows = d["eo"][bass.ds(b * SLOT, SLOT), :].rearrange("(e p) w -> p e w", p=CAP)
                sp.dma_start(rows[0:OW, :, :], o[u][:, :, 0, :]).then_inc(o_out[u], 16)
                sp.dma_start(rows[OW:CAP, :, :], o[u][2 * OW - CAP:OW, :, 1, :]).then_inc(o_out[u], 16)

            pipeline(sp, B, 2, [(0, load), (2, store)])
            for u in range(2):
                sp.wait_ge(o_out[u], 32 * B // 2)

        @block.scalar
        def _(act):
            for e in range(E):
                act.dma_start(wi_a[:, e, :], d["wi_a"][:, e, :]).then_inc(w_in[e], 16)
                act.dma_start(wi_r[:, e, :, :], d["wi_r"][:, e, :, :]).then_inc(w_in[e], 16)
                act.dma_start(wo[:, e, :, :], d["wo"][:, e, :, :]).then_inc(w_in[e], 16)

            def hidden(b, e, u):
                for q in range(0, UP, 2):
                    act.wait_ge(u_mm, UP * (E * b + e) + q + 1)
                    if q == 0:
                        wait(act, d_mm, E * b + e - 1)
                    act.activation(hT[e % 2][:, 2 * q:2 * q + 2, :], h_ps[(e + q) % 2][:, :, 0:CAP],
                                   ACT.Relu).then_inc(h_even, 1)

            over_experts(act, [(E, hidden)])

        @block.tensor
        def _(pe):
            pe.wait_ge(ident_in, 16)

            def turn_(b, e, u):
                if e == 0:
                    pe.wait_ge(x_in[u], 16 * (b - u) + 32)
                for g in groups(e):
                    n = (u + g) % 2
                    wait(pe, t_ready, NG * b + g - 1)
                    cols = [(g // XG, g % XG * 4 + i) for i in range(4)] if g < NG - 1 else [(0, XCH - 1), (1, XCH - 1)]
                    for i, (k, c) in enumerate(cols):
                        mm = pe.transpose(t_ps[n][:, i * XROWS:(i + 1) * XROWS], x[u][:, c, k * DA:(k + 1) * DA],
                                          ident[0:XROWS, 0:XROWS])
                    mm.then_inc(t_mm, 1)

            def up(b, e, u):
                pe.wait_ge(t_ready, NG * (b + 1))
                pe.wait_ge(w_in[e], 48)
                t = slice(e * CAP, (e + 1) * CAP)
                for q in range(UP):
                    if q == 0:
                        wait(pe, h_odd, E * b + e)
                    else:
                        wait(pe, h_even, 2 * (E * b + e) + q - 1)
                    h = h_ps[(e + q) % 2]
                    for i in range(2):
                        m = (2 * q + i) * 128
                        pe.matmul(h[:, i, 0:CAP], wi_a[:, e, m:m + 128], xT[u][:, 0, t], start=True, stop=False)
                    for i in range(2):
                        s = slice(64 * i, 64 * i + 64)
                        mm = pe.matmul(h[:, i, 0:CAP], wi_r[s, e, q, :], xT[u][s, 1, t], start=False, stop=True)
                    mm.then_inc(u_mm, 1)

            def down(b, e, u):
                wait(pe, o_ready, E * b + e - 1)
                pe.wait_ge(h_even, 2 * (E * b + e + 1))
                pe.wait_ge(h_odd, E * b + e + 1)
                for i in range(2):
                    s = i * (CAP - OW)
                    for k in range(FC):
                        mm = pe.matmul(o_ps[e % 2][:, i * D:(i + 1) * D], hT[e % 2][:, k, s:s + OW], wo[:, e, k, :],
                                       start=(k == 0), stop=(k == FC - 1))
                mm.then_inc(d_mm, 1)

            over_experts(pe, [(E, up), (0, turn_), (E + 1, down)])

        @block.vector
        def _(dve):
            def turned(b, e, u):
                if e == 0:
                    wait(dve, u_mm, UP * E * (b - 1))
                for g in groups(e):
                    n = (u + g) % 2
                    dve.wait_ge(t_mm, NG * b + g + 1)
                    if g < NG - 1:
                        c = g % XG * 4 * XROWS
                        i = dve.tensor_copy(xT[u][:, g // XG, c:c + 4 * XROWS], t_ps[n][:, 0:4 * XROWS])
                    else:
                        i = dve.tensor_copy(xT[u][:, :, SLOT - XROWS:SLOT],
                                            t_ps[n][:, 0:2 * XROWS].rearrange("p (k t) -> p k t", k=2))
                    i.then_inc(t_ready, 1)

            def hidden(b, e, u):
                dve.wait_ge(u_mm, UP * (E * b + e) + 2)
                wait(dve, d_mm, E * b + e - 1)
                dve.tensor_scalar(hT[e % 2][:, 2:4, :], h_ps[(e + 1) % 2][:, :, 0:CAP], 0.0, None,
                                  ALU.max).then_inc(h_odd, 1)

            def outputs(b, e, u):
                dve.wait_ge(d_mm, E * b + e + 1)
                if e == 0:
                    wait(dve, o_out[u], 16 * (b - u))
                dve.tensor_copy(o[u][:, e, :, :].rearrange("p i w -> p (i w)"),
                                o_ps[e % 2][:, 0:2 * D]).then_inc(o_ready, 1)

            over_experts(dve, [(E, hidden), (0, turned), (E + 1, outputs)])


def attention(nc, d, keep):
    with ExitStack() as ctx:
        def sb(name, shape, dt=F32):
            return ctx.enter_context(nc.sbuf_tensor("at_" + name, shape, dt))

        count = ctx.enter_context(semaphores(nc))

        def sem(name):
            return count("at_" + name)

        def kept_sem(name):
            return keep.enter_context(nc.semaphore("at_" + name))

        def ps(name, shape):
            return ctx.enter_context(nc.psum_tensor("at_" + name, shape, F32))

        K, TURN = 2 * NC, 4
        wq_a, wk_a = sb("wq_a", [128, D]), sb("wk_a", [128, D])
        wq_r, wk_r = sb("wq_r", [128, D]), sb("wk_r", [128, D])
        wv_a, wv_r = sb("wv_a", [128, D]), sb("wv_r", [128, D])
        qk_b = sb("qk_b", [128, 4])
        v_b = sb("v_b", [TC, 2, D])
        decay = sb("decay", [TC, L])
        ident = sb("ident", [128, 128])
        index = [sb(f"index{i}", [TC, K], I32) for i in range(2)]
        weight = [sb(f"weight{i}", [TC, K]) for i in range(2)]
        h = [sb(f"h{i}", [TC, NC, D]) for i in range(TURN)]
        back = [sb(f"back{i}", [TC, K, D]) for i in range(2)]
        stat, mv = sb("stat", [TC, NC, 6]), sb("mv", [TC, NC, 2])
        root, rstd = sb("root", [TC, NC]), sb("rstd", [TC, NC])
        xn = [sb(f"xn{i}", [TC, NC, 256]) for i in range(2)]
        xT = [sb(f"xT{i}", [128, 2, L]) for i in range(2)]
        qT = [sb("qT_a", [128, L]), sb("qT_r", [DR, L])]
        kT = [sb("kT_a", [128, L]), sb("kT_r", [DR, L])]
        v = [sb(f"v{i}", [TC, NC, D]) for i in range(2)]
        sT = sb("sT", [TC, NC, L])
        t_ps = [ps(f"t_ps{i}", [128, 512]) for i in range(2)]
        p_ps = [ps(f"p_ps{i}", [128, 512]) for i in range(2)]
        proj_ps = [p_ps, t_ps]
        s_ps = [ps(f"s_ps{i}", [TC, 512]) for i in range(2)]
        o_ps = [ps(f"o_ps{i}", [TC, 512]) for i in range(2)]

        loaded = sem("loaded")
        h_in = [sem(f"h_in{i}") for i in range(TURN)]
        table_in = [sem(f"table_in{i}") for i in range(2)]
        back_in = [kept_sem(f"back_in{i}") for i in range(2)]
        h_out = [sem(f"h_out{i}") for i in range(TURN)]
        var_ready, root_ready, norm_ready = sem("var_ready"), sem("root_ready"), sem("norm_ready")
        back_read, out_ready, o_read = sem("back_read"), sem("out_ready"), sem("o_read")
        t_mm, t_ready, p_mm, p_ready = sem("t_mm"), sem("t_ready"), sem("p_mm"), sem("p_ready")
        v_mm, v_ready, s_mm, s_ready, o_mm = sem("v_mm"), sem("v_ready"), sem("s_mm"), sem("s_ready"), sem("o_mm")
        passed, pool_passed = sem("passed"), sem("pool_passed")
        TG, VG = 4, NC // 2
        proj = [((0, 0, DA), (1, 0, DA)), ((0, DA, DR), (1, DA, DR))]
        PG = 4
        pieces = [(c, max(i * HL, c * TC), (i + 1) * HL) for c in range(NC) for i in range(2) if c * TC < (i + 1) * HL]
        SG = len(pieces)
        block = ctx.enter_context(nc.Block())

        @block.sync
        def _(sp):
            consts = ((wq_a, "wq_a"), (wk_a, "wk_a"), (wq_r, "wq_r"), (wk_r, "wk_r"), (wv_a, "wv_a"), (wv_r, "wv_r"),
                      (qk_b, "qk_b"), (decay, "decay"), (ident, "ident"))

            def load(b, u):
                wait_alone(sp, back_read, b - 1, passed)
                sp.dma_start(index[u % 2][:, :], d["rt_index"][bass.ds(b, 1), :, :].rearrange(
                    "o p k -> (o p) k")).then_inc(table_in[u % 2], 16)
                sp.dma_start(weight[u % 2][:, :], d["rt_weight"][bass.ds(b, 1), :, :].rearrange(
                    "o p k -> (o p) k")).then_inc(table_in[u % 2], 16)
                wait_alone(sp, h_out[u], (b - u) * (16 // TURN), passed)
                sp.dma_start(h[u][:, :, :], d["h1"][bass.ds(b, 1), :, :].rearrange(
                    "o (c p) w -> p (o c) w", p=TC)).then_inc(h_in[u], 16)
                if isinstance(b, int) and b == 0:
                    for t, s in consts:
                        sp.dma_start(t[:, :], d[s]).then_inc(loaded, 16)
                    sp.dma_start(v_b[:, :, :], d["v_b"]).then_inc(loaded, 16)

            def store(b, u):
                wait_alone(sp, out_ready, b + 1, passed)
                sp.dma_start(d["h3"][bass.ds(b, 1), :, :].rearrange("o (c p) w -> p (o c) w", p=TC),
                             h[u][:, :, :]).then_inc(h_out[u], 16)

            pipeline(sp, B, TURN, [(0, load), (3, store)])
            for u in range(TURN):
                sp.wait_ge(h_out[u], 16 * B // TURN)

        @block.gpsimd
        def _(pool):
            def gather(b, u):
                wait_alone(pool, table_in[u % 2], 16 * (b - u % 2) + 32, pool_passed)
                wait_alone(pool, back_read, b - 1, pool_passed)
                for k in range(K):
                    pool.indirect_dma_start(
                        out=back[u % 2][:, k, :], out_offset=None, in_=d["eo"],
                        in_offset=bass.IndirectOffsetOnAxis(ap=index[u % 2][:, k:k + 1], axis=0)).then_inc(back_in[u % 2], 16)

            pipeline(pool, B, TURN, [(0, gather)])

        @block.scalar
        def _(act):
            act.wait_ge(loaded, 16 * 10)

            def roots(b, u):
                act.wait_ge(var_ready, b + 1)
                act.activation(root[:, :], mv[:, :, 1], ACT.Sqrt).then_inc(root_ready, 1)

            def turned(b, u):
                wait(act, v_mm, VG * (b - 1))
                for g in range(TG):
                    act.wait_ge(t_mm, TG * b + g + 1)
                    act.activation(xT[u % 2][:, g // 2, g % 2 * HL:(g % 2 + 1) * HL], t_ps[g % 2][:, 0:HL],
                                   ACT.Copy).then_inc(t_ready, 1)

            def projected(b, u):
                wait(act, s_mm, SG * b)
                for g in range(PG):
                    act.wait_ge(p_mm, PG * b + g + 1)
                    for which, m, n in proj[g // 2]:
                        dst = (qT, kT)[which][m // DA]
                        i = act.activation(dst[0:n, g % 2 * HL:(g % 2 + 1) * HL], proj_ps[g % 2][which][0:n, 0:HL],
                                           ACT.Identity, bias=qk_b[0:n, 2 * which + m // DA:2 * which + m // DA + 1])
                    act.drain().then_inc(p_ready, 1)

            pipeline(act, B, TURN, [(2, turned), (2, projected), (1, roots)])

        @block.tensor
        def _(pe):
            pe.wait_ge(loaded, 16 * 10)

            def turn_(b, u):
                pe.wait_ge(norm_ready, b + 1)
                for g in range(TG):
                    if g == 0:
                        wait(pe, p_ready, PG * b)
                    if g >= 2:
                        pe.wait_ge(t_ready, TG * b + g - 1)
                    for i in range(3):
                        c = g % 2 * 3 + i
                        mm = pe.transpose(t_ps[g % 2][:, i * TC:(i + 1) * TC],
                                          xn[u % 2][:, c, g // 2 * DA:(g // 2 + 1) * DA], ident[0:TC, 0:TC])
                    mm.then_inc(t_mm, 1)

            def project(b, u):
                pe.wait_ge(t_ready, TG * (b + 1))
                for g in range(PG):
                    if g < 2:
                        wait(pe, p_ready, PG * b + g - 1)
                    else:
                        pe.wait_ge(p_ready, PG * b + g - 1)
                    t = slice(g % 2 * HL, (g % 2 + 1) * HL)
                    for which, m, n in proj[g // 2]:
                        pe.matmul(proj_ps[g % 2][which][0:n, 0:HL], (wq_a, wk_a)[which][:, m:m + n], xT[u % 2][:, 0, t],
                                  start=True, stop=False)
                    for which, m, n in proj[g // 2]:
                        s = slice(64 * which, 64 * which + 64)
                        mm = pe.matmul(proj_ps[g % 2][which][0:n, 0:HL], (wq_r, wk_r)[which][s, m:m + n], xT[u % 2][s, 1, t],
                                       start=False, stop=True)
                    pe.drain().then_inc(p_mm, 1)

            def values(b, u):
                for g in range(VG):
                    if g < 2:
                        wait(pe, o_read, VG * (b - 2) + g + 2)
                    else:
                        pe.wait_ge(v_ready, VG * b + 1)
                    for i in range(2):
                        c = 2 * g + i
                        t = slice(c * TC, (c + 1) * TC)
                        o = o_ps[g % 2][:, i * D:(i + 1) * D]
                        pe.matmul(o, xT[u % 2][:, 0, t], wv_a[:, :], start=True, stop=False)
                        mm = pe.matmul(o, xT[u % 2][0:DR, 1, t], wv_r[0:DR, :], start=False, stop=True)
                    mm.then_inc(v_mm, 1)

            def scores(b, u):
                pe.wait_ge(p_ready, PG * (b + 1))
                for n, (c, s0, s1) in enumerate(pieces):
                    wait(pe, s_ready, SG * b + n - 1)
                    o = s_ps[(SG * (u % 2) + n) % 2][:, 0:s1 - s0]
                    pe.matmul(o, kT[0][:, c * TC:(c + 1) * TC], qT[0][:, s0:s1], start=True, stop=False)
                    mm = pe.matmul(o, kT[1][:, c * TC:(c + 1) * TC], qT[1][:, s0:s1], start=False, stop=True)
                    mm.then_inc(s_mm, 1)

            def outputs(b, u):
                pe.wait_ge(s_ready, SG * (b + 1))
                pe.wait_ge(v_ready, VG * (b + 1))
                for g in range(VG):
                    if g < 2 and not (isinstance(b, int) and b == B - 1):
                        pe.wait_ge(v_ready, VG * (b + 1) + 2 + g)
                    else:
                        pe.wait_ge(o_read, VG * b + g // 2)
                    for i in range(2):
                        s = 2 * g + i
                        for c in range(s + 1):
                            mm = pe.matmul(o_ps[(g + 1) % 2][:, i * D:(i + 1) * D], sT[:, c, s * TC:(s + 1) * TC],
                                           v[u % 2][:, c, :], start=(c == 0), stop=(c == s))
                    mm.then_inc(o_mm, 1)

            pipeline(pe, B, TURN, [(2, turn_), (3, scores), (2, project), (2, values), (3, outputs)])

        @block.vector
        def _(dve):
            dve.wait_ge(loaded, 16 * 10)

            def combine(b, u):
                dve.wait_ge(h_in[u], (b - u) * (16 // TURN) + 16)
                dve.wait_ge(back_in[u % 2], K * 8 * (b - u % 2) + K * 16)
                for k in range(K):
                    if k == NC:
                        dve.drain()
                    x = h[u][:, k % NC, :]
                    dve.scalar_tensor_tensor(out=x, in0=back[u % 2][:, k, :], scalar=weight[u % 2][:, k:k + 1], in1=x,
                                             op0=ALU.mult, op1=ALU.add)
                dve.drain().then_inc(back_read, 1)
                statistics(dve, h[u], stat, mv).then_inc(var_ready, 1)

            def normalize(b, u):
                dve.wait_ge(root_ready, b + 1)
                dve.reciprocal(rstd[:, :], root[:, :])
                dve.drain()
                wait(dve, t_mm, TG * (b - 1))
                for c in range(NC):
                    m, r = mv[:, c, 0:1], rstd[:, c:c + 1]
                    dve.tensor_scalar(xn[u % 2][:, c, 0:D], h[u][:, c, :], m, r, ALU.subtract, ALU.mult)
                    dve.tensor_scalar(xn[u % 2][:, c, D:256], h[u][:, c, DA:D], m, r, ALU.subtract, ALU.mult)
                dve.drain().then_inc(norm_ready, 1)

            def masked(b, u):
                wait(dve, o_mm, VG * b)
                for n, (c, s0, s1) in enumerate(pieces):
                    dve.wait_ge(s_mm, SG * b + n + 1)
                    dve.tensor_tensor(sT[:, c, s0:s1], s_ps[(SG * (u % 2) + n) % 2][:, 0:s1 - s0],
                                      decay[:, s0 - c * TC:s1 - c * TC], ALU.mult).then_inc(s_ready, 1)

            def values(b, u):
                wait(dve, o_mm, VG * (b - 1))
                for g in range(VG):
                    dve.wait_ge(v_mm, VG * b + g + 1)
                    dve.tensor_tensor(v[u % 2][:, 2 * g:2 * g + 2, :],
                                      o_ps[g % 2][:, 0:2 * D].rearrange("p (i w) -> p i w", i=2), v_b[:, :, :],
                                      ALU.add).then_inc(v_ready, 1)

            def outputs(b, u):
                for g in range(VG):
                    dve.wait_ge(o_mm, VG * b + g + 1)
                    x = h[u][:, 2 * g:2 * g + 2, :].rearrange("p c w -> p (c w)")
                    dve.tensor_tensor(x, x, o_ps[(g + 1) % 2][:, 0:2 * D], ALU.add).then_inc(o_read, 1)
                dve.drain().then_inc(out_ready, 1)

            pipeline(dve, B, TURN, [(3, masked), (1, combine), (2, values), (1, normalize), (3, outputs)])


def class_weights(nc, keep):
    def sb(name, shape):
        return keep.enter_context(nc.sbuf_tensor("cl_" + name, shape, F32))

    return {"a1_a": sb("a1_a", [128, NA, F]), "a1_r": sb("a1_r", [DR, NA, F]), "a2": sb("a2", [128, NA, FC, D]),
            "loaded": nc.alloc_semaphore(name="cl_weights_in")}


def patch_ffn(nc, d, classes):
    TURN = 4
    with ExitStack() as ctx:
        def sb(name, shape, dt=F32):
            return ctx.enter_context(nc.sbuf_tensor("ff_" + name, shape, dt))

        count = ctx.enter_context(semaphores(nc))

        def sem(name):
            return count("ff_" + name)

        def ps(name, shape):
            return ctx.enter_context(nc.psum_tensor("ff_" + name, shape, F32))

        UP, OG, TG = FC // 2, NC // 2, 4
        w1_a, w1_r = sb("w1_a", [128, F]), sb("w1_r", [128, UP, 128])
        b1 = sb("b1", [128, FC])
        w2 = sb("w2", [128, FC, D])
        b2 = sb("b2", [TC, NC, D])
        ident = sb("ident", [128, 128])
        h = [sb(f"h{i}", [TC, NC, D]) for i in range(TURN)]
        stat, mv = sb("stat", [TC, NC, 6]), sb("mv", [TC, NC, 2])
        root, rstd = sb("root", [TC, NC]), sb("rstd", [TC, NC])
        xn = [sb(f"xn{i}", [TC, NC, 256]) for i in range(2)]
        xT = [sb(f"xT{i}", [128, 2, L]) for i in range(2)]
        hT = sb("hT", [128, FC, L])
        t_ps = [ps(f"t_ps{i}", [128, 512]) for i in range(2)]
        u_ps = [ps(f"u_ps{i}", [128, 2, 512]) for i in range(2)]
        o_ps = [ps(f"o_ps{i}", [TC, 512]) for i in range(2)]

        loaded = sem("loaded")
        h_in = [sem(f"h_in{i}") for i in range(TURN)]
        h_out = [sem(f"h_out{i}") for i in range(TURN)]
        var_ready, root_ready, norm_ready = sem("var_ready"), sem("root_ready"), sem("norm_ready")
        biased, out_ready, o_read = sem("biased"), sem("out_ready"), sem("o_read")
        t_mm, t_ready, u_mm, hid_ready, o_mm = sem("t_mm"), sem("t_ready"), sem("u_mm"), sem("hid_ready"), sem("o_mm")
        passed = sem("passed")
        UG = 2 * UP
        block = ctx.enter_context(nc.Block())

        @block.sync
        def _(sp):
            def load(b, u):
                wait_alone(sp, h_out[u], (b - u) * (32 // TURN), passed)
                sp.dma_start(h[u][:, :, :], d["h3"][bass.ds(b, 1), :, :].rearrange(
                    "o (c p) w -> p (o c) w", p=TC)).then_inc(h_in[u], 16)
                if isinstance(b, int) and b == 0:
                    sp.dma_start(ident[:, :], d["ident"]).then_inc(loaded, 16)
                    sp.dma_start(w1_a[:, :], d["w1_a"]).then_inc(loaded, 16)
                    sp.dma_start(w1_r[:, :, :], d["w1_r"]).then_inc(loaded, 16)
                    sp.dma_start(b1[:, :], d["b1"]).then_inc(loaded, 16)
                    sp.dma_start(w2[:, :, :], d["w2"]).then_inc(loaded, 16)
                    sp.dma_start(b2[:, :, :], d["b2"]).then_inc(loaded, 16)
                if isinstance(b, int) and b == TURN - 1:
                    sp.dma_start(classes["a1_a"][:, :, :], d["a1_a"]).then_inc(classes["loaded"], 16)
                    sp.dma_start(classes["a1_r"][:, :, :], d["a1_r"]).then_inc(classes["loaded"], 16)
                    sp.dma_start(classes["a2"][:, :, :, :], d["a2"]).then_inc(classes["loaded"], 16)

            def store(b, u):
                wait_alone(sp, out_ready, b + 1, passed)
                rows = d["out"][bass.ds(b, 1), :, :].rearrange("o (c p) w -> p (o c) w", p=TC)
                sp.dma_start(rows[NCLS:TC, 0:1, :], h[u][NCLS:TC, 0:1, :]).then_inc(h_out[u], 16)
                sp.dma_start(rows[:, 1:NC, :], h[u][:, 1:NC, :]).then_inc(h_out[u], 16)

            pipeline(sp, B, TURN, [(0, load), (3, store)])
            for u in range(TURN):
                sp.wait_ge(h_out[u], 32 * B // TURN)

        @block.gpsimd
        def _(pool):
            pool.wait_ge(loaded, 16 * 6)

            def bias(b, u):
                wait_alone(pool, norm_ready, b + 1, passed)
                pool.tensor_tensor(h[u][:, :, :], h[u][:, :, :], b2[:, :, :], ALU.add).then_inc(biased, 1)

            pipeline(pool, B, TURN, [(1, bias)])

        @block.scalar
        def _(act):
            act.wait_ge(loaded, 16 * 6)

            def roots(b, u):
                act.wait_ge(var_ready, b + 1)
                act.activation(root[:, :], mv[:, :, 1], ACT.Sqrt).then_inc(root_ready, 1)

            def hidden(b, u):
                wait(act, o_mm, OG * b)
                for g in range(UG):
                    act.wait_ge(u_mm, UG * b + g + 1)
                    half, q = g // UP, g % UP
                    for i in range(2):
                        m = 2 * q + i
                        act.activation(hT[:, m, half * HL:(half + 1) * HL], u_ps[g % 2][:, i, 0:HL],
                                       ACT.Gelu, bias=b1[:, m:m + 1])
                    act.drain().then_inc(hid_ready, 1)

            pipeline(act, B, TURN, [(1, roots), (2, hidden)])

        @block.tensor
        def _(pe):
            pe.wait_ge(loaded, 16 * 6)

            def turn_(b, u):
                pe.wait_ge(norm_ready, b + 1)
                for g in range(TG):
                    wait(pe, t_ready, TG * b + g - 1)
                    for i in range(3):
                        c = g % 2 * 3 + i
                        mm = pe.transpose(t_ps[g % 2][:, i * TC:(i + 1) * TC],
                                          xn[u % 2][:, c, g // 2 * DA:(g // 2 + 1) * DA], ident[0:TC, 0:TC])
                    mm.then_inc(t_mm, 1)

            def up(b, u):
                pe.wait_ge(t_ready, TG * (b + 1))
                for g in range(UG):
                    wait(pe, hid_ready, UG * b + g - 1)
                    t, q = slice(g // UP * HL, (g // UP + 1) * HL), g % UP
                    for i in range(2):
                        m = (2 * q + i) * 128
                        pe.matmul(u_ps[g % 2][:, i, 0:HL], w1_a[:, m:m + 128], xT[u % 2][:, 0, t], start=True, stop=False)
                    for i in range(2):
                        s = slice(64 * i, 64 * i + 64)
                        mm = pe.matmul(u_ps[g % 2][:, i, 0:HL], w1_r[s, q, :], xT[u % 2][s, 1, t], start=False, stop=True)
                    mm.then_inc(u_mm, 1)

            def down(b, u):
                pe.wait_ge(hid_ready, UG * (b + 1))
                for g in range(OG):
                    wait(pe, o_read, OG * b + g - 1)
                    for i in range(2):
                        c = 2 * g + i
                        for k in range(FC):
                            mm = pe.matmul(o_ps[(OG * u + g) % 2][:, i * D:(i + 1) * D], hT[:, k, c * TC:(c + 1) * TC],
                                           w2[:, k, :], start=(k == 0), stop=(k == FC - 1))
                    mm.then_inc(o_mm, 1)

            pipeline(pe, B, TURN, [(2, turn_), (3, down), (2, up)])

        @block.vector
        def _(dve):
            dve.wait_ge(loaded, 16 * 6)

            def normalize(b, u):
                dve.wait_ge(h_in[u], (b - u) * (16 // TURN) + 16)
                statistics(dve, h[u], stat, mv).then_inc(var_ready, 1)
                dve.wait_ge(root_ready, b + 1)
                dve.reciprocal(rstd[:, :], root[:, :])
                dve.drain()
                wait(dve, t_mm, TG * (b - 1))
                for c in range(NC):
                    m, r = mv[:, c, 0:1], rstd[:, c:c + 1]
                    dve.tensor_scalar(xn[u % 2][:, c, 0:D], h[u][:, c, :], m, r, ALU.subtract, ALU.mult)
                    dve.tensor_scalar(xn[u % 2][:, c, D:256], h[u][:, c, DA:D], m, r, ALU.subtract, ALU.mult)
                dve.drain().then_inc(norm_ready, 1)

            def turned(b, u):
                wait(dve, u_mm, UG * (b - 1))
                for g in range(TG):
                    dve.wait_ge(t_mm, TG * b + g + 1)
                    dve.tensor_copy(xT[u % 2][:, g // 2, g % 2 * HL:(g % 2 + 1) * HL],
                                    t_ps[g % 2][:, 0:HL]).then_inc(t_ready, 1)

            def outputs(b, u):
                dve.wait_ge(biased, b + 1)
                for g in range(OG):
                    dve.wait_ge(o_mm, OG * b + g + 1)
                    x = h[u][:, 2 * g:2 * g + 2, :].rearrange("p c w -> p (c w)")
                    dve.tensor_tensor(x, x, o_ps[(OG * u + g) % 2][:, 0:2 * D], ALU.add).then_inc(o_read, 1)
                dve.drain().then_inc(out_ready, 1)

            pipeline(dve, B, TURN, [(2, turned), (1, normalize), (3, outputs)])


def class_ffn(nc, d, classes):
    N = NCLS * B
    with ExitStack() as ctx:
        def sb(name, shape, dt=F32):
            return ctx.enter_context(nc.sbuf_tensor("cl_" + name, shape, dt))

        count = ctx.enter_context(semaphores(nc))

        def sem(name):
            return count("cl_" + name)

        def ps(name, shape):
            return ctx.enter_context(nc.psum_tensor("cl_" + name, shape, F32))

        a1_a, a1_r, a2 = classes["a1_a"], classes["a1_r"], classes["a2"]
        a1_b, a2_b = sb("a1_b", [128, NA, FC]), sb("a2_b", [NA, D])
        gw_a, gw_r = sb("gw_a", [128, 2, NCLS]), sb("gw_r", [DR, 2, NCLS])
        own = sb("own", [N, 2, NCLS])
        adapter = sb("adapter", [N, 2, NA])
        ident, ones = sb("ident", [128, 128]), sb("ones", [N, 128])
        h, xn = sb("h", [N, D]), sb("xn", [N, D])
        stat, mv = sb("stat", [N, 6]), sb("mv", [N, 2])
        root, rstd = sb("root", [N, 1]), sb("rstd", [N, 1])
        x_a, x_r = sb("x_a", [128, N]), sb("x_r", [DR, N])
        picked, logit, expo = sb("picked", [N, 2, NCLS]), sb("logit", [N, 2]), sb("expo", [N, 2])
        top, low, total = sb("top", [N, 1]), sb("low", [N, 1]), sb("total", [N, 1])
        gate, chosen, kept = sb("gate", [N, 2]), sb("chosen", [N, 2]), sb("kept", [N, 2])
        per_adapter, gate_c = sb("per_adapter", [N, 2, NA]), sb("gate_c", [N, NA])
        gate_cT = sb("gate_cT", [NA, N])
        diag = sb("diag", [N, 2, N])
        wide = sb("wide", [128, 2, N])
        gel = sb("gel", [128, NA, FC, N])
        hid = sb("hid", [128, NA, FC, N])
        t_ps, g_ps, c_ps = ps("t_ps", [128, 512]), ps("g_ps", [128, 512]), ps("c_ps", [128, 512])
        w_ps, o_ps = ps("w_ps", [128, 512]), ps("o_ps", [N, 512])
        u_ps = [ps(f"u_ps{i}", [128, 512]) for i in range(3)]

        loaded, consts_in = sem("loaded"), sem("consts_in")
        var_ready, root_ready, norm_ready = sem("var_ready"), sem("root_ready"), sem("norm_ready")
        x_mm, x_ready, g_mm, logit_ready, exp_ready = sem("x_mm"), sem("x_ready"), sem("g_mm"), sem("logit_ready"), sem("exp_ready")
        gates_ready, gates_mm, gates_wide = sem("gates_ready"), sem("gates_mm"), sem("gates_wide")
        u_mm, gel_ready, hid_ready, o_mm = sem("u_mm"), sem("gel_ready"), sem("hid_ready"), sem("o_mm")
        out_ready, stored = sem("out_ready"), sem("stored")
        G = 4
        ups = [(a, m0, min(G, FC - m0)) for a in range(NA) for m0 in range(0, FC, G)]
        block = ctx.enter_context(nc.Block())

        @block.sync
        def _(sp):
            for i in range(NCLS):
                sp.dma_start(h[i * B:(i + 1) * B, :], d["h3"][:, i, :]).then_inc(loaded, 16)
            for t, s in ((ident, "ident"), (a2_b, "a2_b")):
                sp.dma_start(t[:, :], d[s]).then_inc(consts_in, 16)
            for t, s in ((gw_a, "gw_a"), (gw_r, "gw_r"), (own, "own"), (adapter, "adapter"), (a1_b, "a1_b")):
                sp.dma_start(t[:, :, :], d[s]).then_inc(consts_in, 16)
            sp.wait_ge(out_ready, 1)
            for i in range(NCLS):
                sp.dma_start(d["out"][:, i, :], h[i * B:(i + 1) * B, :]).then_inc(stored, 16)
            sp.wait_ge(stored, 16 * NCLS)

        @block.scalar
        def _(act):
            act.wait_ge(consts_in, 16 * 7)
            act.wait_ge(var_ready, 1)
            act.activation(root[:, :], mv[:, 1:2], ACT.Sqrt).then_inc(root_ready, 1)
            act.wait_ge(logit_ready, 1)
            act.activation(expo[:, :], logit[:, :], ACT.Exp).then_inc(exp_ready, 1)
            for n, (a, m0, k) in enumerate(ups):
                act.wait_ge(u_mm, n + 1)
                for i in range(k):
                    act.activation(gel[:, a, m0 + i, :], u_ps[n % 3][:, i * N:(i + 1) * N], ACT.Gelu,
                                   bias=a1_b[:, a, m0 + i:m0 + i + 1])
                act.drain().then_inc(gel_ready, 1)

        @block.tensor
        def _(pe):
            pe.wait_ge(consts_in, 16 * 7)
            pe.wait_ge(norm_ready, 1)
            pe.transpose(t_ps[:, 0:N], xn[:, 0:DA], ident[0:N, 0:N])
            pe.transpose(t_ps[0:DR, N:2 * N], xn[:, DA:D], ident[0:N, 0:N]).then_inc(x_mm, 1)
            pe.wait_ge(x_ready, 1)
            pe.matmul(g_ps[0:N, 0:2 * NCLS], x_a[:, :], gw_a[:, :, :], start=True, stop=False)
            pe.matmul(g_ps[0:N, 0:2 * NCLS], x_r[:, :], gw_r[:, :, :], start=False, stop=True).then_inc(g_mm, 1)
            pe.wait_ge(classes["loaded"], 48)
            for n, (a, m0, k) in enumerate(ups):
                wait(pe, gel_ready, n - 2)
                for i in range(k):
                    m, o = (m0 + i) * 128, u_ps[n % 3][:, i * N:(i + 1) * N]
                    pe.matmul(o, a1_a[:, a, m:m + 128], x_a[:, :], start=True, stop=False)
                    mm = pe.matmul(o, a1_r[:, a, m:m + 128], x_r[:, :], start=False, stop=True)
                mm.then_inc(u_mm, 1)
            pe.wait_ge(gates_ready, 1)
            pe.matmul(w_ps[:, 0:2 * N], ones[:, :], diag[:, :, :], start=True, stop=True)
            pe.transpose(c_ps[0:NA, 0:N], gate_c[:, :], ident[0:N, 0:N]).then_inc(gates_mm, 1)
            pe.wait_ge(gates_wide, 1)
            pe.matmul(o_ps[:, 0:D], gate_cT[:, :], a2_b[:, :], start=True, stop=False)
            for c in range(NA):
                pe.wait_ge(hid_ready, 1)
                for m in range(FC):
                    mm = pe.matmul(o_ps[:, 0:D], hid[:, c, m, :], a2[:, c, m, :], start=False,
                                   stop=(c == NA - 1 and m == FC - 1))
            mm.then_inc(o_mm, 1)

        @block.vector
        def _(dve):
            dve.memset(ones[:, :], 1.0)
            dve.memset(hid[:, :, :, :], 0.0)
            dve.wait_ge(consts_in, 16 * 7)
            dve.wait_ge(loaded, 16 * NCLS)
            dve.bn_stats(stat[:, :], h[:, :])
            dve.drain()
            dve.bn_aggr(mv[:, :], stat[:, :])
            dve.drain()
            dve.tensor_scalar(mv[:, 1:2], mv[:, 1:2], EPS, None, ALU.add).then_inc(var_ready, 1)
            dve.wait_ge(root_ready, 1)
            dve.reciprocal(rstd[:, :], root[:, :])
            dve.drain()
            dve.tensor_scalar(xn[:, :], h[:, :], mv[:, 0:1], rstd[:, :], ALU.subtract, ALU.mult).then_inc(norm_ready, 1)
            dve.wait_ge(x_mm, 1)
            dve.tensor_copy(x_a[:, :], t_ps[:, 0:N])
            dve.tensor_copy(x_r[:, :], t_ps[0:DR, N:2 * N])
            dve.drain().then_inc(x_ready, 1)
            dve.wait_ge(g_mm, 1)
            dve.tensor_tensor(picked[:, :, :], own[:, :, :],
                              g_ps[0:N, 0:2 * NCLS].rearrange("p (e i) -> p e i", e=2), ALU.mult)
            dve.drain()
            dve.tensor_reduce(logit[:, :], picked[:, :, :], AX.X, ALU.add)
            dve.drain()
            dve.tensor_reduce(top[:, :], logit[:, :], AX.X, ALU.max)
            dve.drain()
            dve.tensor_scalar(logit[:, :], logit[:, :], top[:, :], None, ALU.subtract).then_inc(logit_ready, 1)
            dve.wait_ge(exp_ready, 1)
            dve.tensor_reduce(total[:, :], expo[:, :], AX.X, ALU.add)
            dve.drain()
            dve.reciprocal(total[:, :], total[:, :])
            dve.drain()
            dve.tensor_scalar(gate[:, :], expo[:, :], total[:, :], None, ALU.mult)
            dve.drain()
            dve.tensor_reduce(low[:, :], gate[:, :], AX.X, ALU.min)
            dve.drain()
            dve.tensor_scalar(chosen[:, :], gate[:, :], low[:, :], None, ALU.is_gt)
            dve.drain()
            dve.tensor_tensor(kept[:, :], gate[:, :], chosen[:, :], ALU.mult)
            dve.drain()
            dve.tensor_reduce(total[:, :], kept[:, :], AX.X, ALU.add)
            dve.drain()
            dve.tensor_scalar(total[:, :], total[:, :], 1e-6, None, ALU.max)
            dve.drain()
            dve.reciprocal(total[:, :], total[:, :])
            dve.drain()
            dve.tensor_scalar(kept[:, :], kept[:, :], total[:, :], None, ALU.mult)
            dve.drain()
            for e in range(2):
                dve.tensor_scalar(diag[:, e, :], ident[0:N, 0:N], kept[:, e:e + 1], None, ALU.mult)
                dve.tensor_scalar(per_adapter[:, e, :], adapter[:, e, :], kept[:, e:e + 1], None, ALU.mult)
            dve.drain()
            dve.tensor_tensor(gate_c[:, :], per_adapter[:, 0, :], per_adapter[:, 1, :], ALU.add)
            dve.drain().then_inc(gates_ready, 1)
            dve.wait_ge(gates_mm, 1)
            dve.tensor_copy(wide[:, :, :], w_ps[:, 0:2 * N].rearrange("p (e t) -> p e t", e=2))
            dve.tensor_copy(gate_cT[:, :], c_ps[0:NA, 0:N])
            dve.drain().then_inc(gates_wide, 1)
            dve.wait_ge(gel_ready, len(ups))
            for i in range(NCLS):
                for e in range(2):
                    a, c = PAIRS[i][e]
                    t = slice(i * B, (i + 1) * B)
                    dve.tensor_tensor(hid[:, c, :, t], gel[:, a, :, t],
                                      wide[:, e, t].unsqueeze(1).to_broadcast([128, FC, B]), ALU.mult)
            dve.drain().then_inc(hid_ready, 1)
            dve.wait_ge(o_mm, 1)
            dve.tensor_tensor(h[:, :], h[:, :], o_ps[:, 0:D], ALU.add).then_inc(out_ready, 1)


def lay_out(a):
    f = np.float32
    o = {}
    x = a["x"].reshape(B, 3, IMG, 4, IMG, 4)
    o["patches"] = np.ascontiguousarray(x.transpose(0, 1, 3, 5, 2, 4).reshape(B, 48, IMG, IMG))
    frame = np.zeros((STEM_K, 2 * ENT, PADW), f)
    frame[0, 1:1 + IMG, 1:1 + IMG] = 1.0
    frame[0, ENT:ENT + IMG, 1:1 + IMG] = 1.0
    o["patch_frame"] = frame
    w = np.zeros((STEM_K, CIN), f)
    w[1:49] = a["L0_tok_stem_w"].reshape(CIN, 48).T
    o["stem_w"] = w
    for n, k, bias in (("bn1", "bn1", "stem_b"), ("bn2", "bn2", "dcn_b")):
        o[n] = np.stack([a["L0_tok_" + bias]] + [a[f"L0_tok_{k}_{c}"] for c in "gbmv"])[None]
    o["off_w"] = np.ascontiguousarray(
        a["L0_tok_off_w"].reshape(TAPS, 2, CIN, TAPS).transpose(2, 3, 1, 0).reshape(CIN, TAPS, 32))
    o["off_b"] = np.ascontiguousarray(a["L0_tok_off_b"].reshape(TAPS, 2).T.reshape(1, 32))
    w = a["L0_tok_dcn_w"].reshape(COUT, CIN, TAPS).transpose(2, 1, 0).reshape(12, 128, COUT)
    o["dcn_w"] = np.ascontiguousarray(w.transpose(1, 0, 2))
    grid = np.zeros((POS, 2, 2, TAPS), f)
    p, half, t = np.arange(POS), np.arange(2), np.arange(TAPS)
    grid[:, :, 0, :] = 4 * (7 * half[None, :, None] + p[:, None, None] // 14) + t[None, None, :] // 4
    grid[:, :, 1, :] = 4 * (p[:, None, None] % 14) + t[None, None, :] % 4
    o["grid"] = grid
    o["ident"] = np.eye(128, dtype=f)
    o["token_ids"] = np.ascontiguousarray(a["x_txt"].reshape(TCOL, 128).T)
    o["circuit"] = a["L0_txt_quantum_params"].reshape(-1, 6 * NQ)
    o["post"] = np.concatenate([a["L0_txt_post_w"].T, a["L0_txt_post_b"][None]])
    def rest(w):
        return np.concatenate([w[DA:], w[DA:]])
    w_bc = np.tile(a["L0_attn_W_x"], (1, 3))
    for n, w in (("w_in", a["L0_attn_W_in"]), ("w_dt", a["L0_attn_W_dt"]), ("w_bc", w_bc)):
        o[n + "_a"], o[n + "_r"] = np.ascontiguousarray(w[:DA]), rest(w)
    chan = np.concatenate([a["L0_attn_conv_w"], a["L0_attn_conv_b"][:, None], a["L0_attn_b_dt"][:, None]], 1)
    o["chan"] = np.stack([chan[:DA], chan[:DA], rest(chan)], 1)
    part = np.zeros((96, 2), f)
    part[32:, 0] = -1.0
    part[64:, 1] = -1.0
    o["part"] = part
    al = a["L0_attn_A_log"]
    o["a_log"] = np.stack([al[:DA], al[:DA], rest(al)], 1)
    dd = a["L0_attn_D"]
    o["skip"] = np.stack([dd[:DA], dd[:DA], rest(dd)], 1)
    o["own_row"] = np.tile(np.eye(2 * NS, dtype=f), (3, 1))
    w = a["L0_attn_W_out"]
    o["w_out_a"], o["w_out_r"] = w[:DA], rest(w)
    w = a["L0_ffn_w_router"]
    o["router_a"], o["router_r"] = w[:DA], w[DA:]
    o["upper"] = np.triu(np.ones((TC, TC), f))
    o["rank"] = np.broadcast_to((E - np.arange(E)).astype(f), (TC, NC, E)).copy()
    o["first_slot"] = np.broadcast_to((CAP * np.arange(E)).astype(f), (TC, 2 * NC, E)).copy()
    o["trash"] = (B * SLOT + np.arange(2 * NC)[None] * TC + np.arange(TC)[:, None]).astype(f)
    w = a["L0_ffn_wi"]
    o["wi_a"] = np.ascontiguousarray(w[:, :DA].transpose(1, 0, 2))
    w = w[:, DA:].reshape(E, DR, FC // 2, 2, 128)
    o["wi_r"] = np.ascontiguousarray(w.transpose(3, 1, 0, 2, 4).reshape(128, E, FC // 2, 128))
    o["wo"] = np.ascontiguousarray(a["L0_ffn_wo"].reshape(E, FC, 128, D).transpose(2, 0, 1, 3))
    w = a["L1_attn_W_qkv"].T
    for i, n in enumerate(("wq", "wk", "wv")):
        o[n + "_a"], o[n + "_r"] = w[:DA, i * D:(i + 1) * D], rest(w[:, i * D:(i + 1) * D])
    bias = a["L1_attn_b_qkv"]
    qk_b = np.zeros((128, 4), f)
    for i in range(2):
        qk_b[:, 2 * i], qk_b[:DR, 2 * i + 1] = bias[i * D:i * D + DA], bias[i * D + DA:(i + 1) * D]
    o["qk_b"] = qk_b
    o["v_b"] = np.broadcast_to(bias[2 * D:], (TC, 2, D))
    diff = np.arange(L)[None] - np.arange(TC)[:, None]
    o["decay"] = np.where(diff >= 0, 0.99 ** np.maximum(diff, 0) / np.sqrt(D), 0).astype(f)
    w = a["L1_ffn_moe0_W1"]
    o["w1_a"] = w[:DA]
    o["w1_r"] = w[DA:].reshape(DR, FC // 2, 2, 128).transpose(2, 0, 1, 3).reshape(128, FC // 2, 128)
    o["b1"] = a["L1_ffn_moe0_b1"].reshape(FC, 128).T
    o["w2"] = a["L1_ffn_moe0_W2"].reshape(FC, 128, D).transpose(1, 0, 2)
    o["b2"] = np.broadcast_to(a["L1_ffn_moe0_b2"], (TC, NC, D))
    w = a["L1_ffn_A1_W"].transpose(1, 0, 2)
    o["a1_a"], o["a1_r"] = w[:DA], w[DA:]
    o["a1_b"] = a["L1_ffn_A1_b"].reshape(NA, FC, 128).transpose(2, 0, 1)
    o["a2"] = a["L1_ffn_A2_W"].reshape(NA, FC, 128, D).transpose(2, 0, 1, 3)
    o["a2_b"] = a["L1_ffn_A2_b"]
    w = a["L1_ffn_G_W"].transpose(1, 2, 0)
    o["gw_a"], o["gw_r"] = w[:DA], w[DA:]
    own, adapter = np.zeros((NCLS, B, 2, NCLS), f), np.zeros((NCLS, B, 2, NA), f)
    for i in range(NCLS):
        own[i, :, :, i] = 1.0
        for e in range(2):
            adapter[i, :, e, PAIRS[i][e][1]] = 1.0
    o["own"], o["adapter"] = own.reshape(NCLS * B, 2, NCLS), adapter.reshape(NCLS * B, 2, NA)
    return {n: np.ascontiguousarray(v) for n, v in o.items()}


SCRATCH = {
    "corner_table0": ((ENT * ENT, 2, 2 * CIN), F32),
    "corner_table1": ((ENT * ENT, 2, 2 * CIN), F32),
    "ssm_x": ((3 * B // 2, 128, L), F32),
    "ssm_z": ((3 * B // 2, 128, L), F32),
    "ssm_dt": ((3 * B // 2, 128, L), F32),
    "ssm_bc": ((B, 96, L), BF16),
    "ssm_y": ((3 * B // 2, 128, L), F32),
    "h1": ((B, L, D), F32),
    "xin": ((B * (SLOT + TRASH), D), F32),
    "rt_index": ((B, TC, 2 * NC), I32),
    "rt_weight": ((B, TC, 2 * NC), F32),
    "eo": ((B * SLOT, D), F32),
    "h3": ((B, L, D), F32),
    "h0": ((B, L, D), F32),
}


def program(nc, d):
    with ExitStack() as keep:
        with ExitStack() as start:
            text = text_parameters(nc, start)
            tokenizer(nc, d, keep, text)
            text_tokens(nc, d, text)
        ssm_inputs(nc, d, keep)
        ssm_scan(nc, d)
        route(nc, d, keep)
        experts(nc, d)
        attention(nc, d, keep)
        classes = class_weights(nc, keep)
        patch_ffn(nc, d, classes)
        class_ffn(nc, d, classes)


def kernel(**inputs):
    import concourse.bacc as bacc
    from concourse.bass_utils import run_bass_kernel_spmd

    nc = bacc.Bacc("TRN2", target_bir_lowering=False, num_devices=1)
    arrays = lay_out({n: np.asarray(v) for n, v in inputs.items()})
    d = {n: nc.dram_tensor("in_" + n, v.shape, mybir.dt.from_np(v.dtype), kind="ExternalInput").ap()
         for n, v in arrays.items()}
    for n, (shape, dt) in SCRATCH.items():
        d[n] = nc.dram_tensor(n, shape, dt, kind="Internal").ap()
    d["out"] = nc.dram_tensor("out", (B, L, D), F32, kind="ExternalOutput").ap()
    program(nc, d)
    r = run_bass_kernel_spmd(nc, [{"in_" + n: v for n, v in arrays.items()}], core_ids=[0])
    return r.results[0]["out"]
```
